# Optimizing a Trainium2 kernel written in Bass

```python
import numpy as np
import jax
import jax.numpy as jnp

def _softmax(x, axis=-1):
    return jax.nn.softmax(x, axis=axis)

def _gelu(x):
    return jax.nn.gelu(x, approximate=True)

def _silu(x):
    return jax.nn.silu(x)

def _sigmoid(x):
    return jax.nn.sigmoid(x)

def _layernorm(x, axis=-1, eps=1e-05):
    m = jnp.mean(x, axis=axis, keepdims=True)
    v = jnp.var(x, axis=axis, keepdims=True)
    return (x - m) / jnp.sqrt(v + eps)

def _scatter_add(tgt, idx, src, axis=0):
    return tgt.at[idx].add(src)

def _segment_sum(src, seg, n):
    return jax.ops.segment_sum(src, seg, n)
kernel_name = 'mk_xattn_ffn_d1_seqx_r8_e49411'

def setup_inputs(seed: int=0):
    np.random.seed(seed)
    _w = jnp.asarray

    def _rec_inputs():
        import jax
        import jax.numpy as jnp
        _rk = jax.random.key(seed)
        x = -0.000125 + 0.9999 * jax.random.normal(jax.random.fold_in(_rk, 1), (8, 256, 128), jnp.float32)
        _lenS = 256 - jax.random.randint(jax.random.fold_in(_rk, 7), (8,), 0, max(1, 256 // 4) + 1, jnp.int32)
        _lenS2 = 256 - jax.random.randint(jax.random.fold_in(_rk, 8), (8,), 0, max(1, 256 // 4) + 1, jnp.int32)
        _ctx_768P = jax.random.normal(jax.random.fold_in(_rk, 11), (8, 16, 96), jnp.float32)
        _ctx_768c = jax.random.dirichlet(jax.random.fold_in(_rk, 511), 0.3 * jnp.ones((16,), jnp.float32), (8, 256))
        _ctx_768t = jnp.einsum('bsk,bkd->bsd', _ctx_768c, _ctx_768P)
        _ctx_768t = _ctx_768t * jax.lax.rsqrt(jnp.mean(jnp.square(_ctx_768t)) + 1e-12) * 0.953939
        ctx_768 = -5.15168e-05 + 0.999825 * (_ctx_768t + 0.3 * jax.random.normal(jax.random.fold_in(_rk, 611), (8, 256, 96), jnp.float32))
        return (x, ctx_768)
    x, ctx_768 = _rec_inputs()

    def _L0_xattn_setup():
        import jax, jax.numpy as jnp
        import numpy as np
        EPS = 1e-05
        key = jax.random.key(seed)
        ks = jax.random.split(key, 6)
        B, Nq, Nk, Dq, Dk = (16, 256, 256, 128, 96)
        s = lambda d: 1.0 / np.sqrt(d)
        return {'q': jax.random.normal(ks[0], (B, Nq, Dq), dtype=jnp.float32), 'k': jax.random.normal(ks[1], (B, Nk, Dk), dtype=jnp.float32), 'Wq': jax.random.normal(ks[2], (Dq, Dq), dtype=jnp.float32) * s(Dq), 'Wk': jax.random.normal(ks[3], (Dq, Dk), dtype=jnp.float32) * s(Dk), 'Wv': jax.random.normal(ks[4], (Dq, Dk), dtype=jnp.float32) * s(Dk), 'Wo': jax.random.normal(ks[5], (Dq, Dq), dtype=jnp.float32) * s(Dq)}
    _L0_xattn_all = _L0_xattn_setup()
    _L0_xattn_in = {k: v for k, v in _L0_xattn_all.items() if k in ('Wq', 'Wk', 'Wv', 'Wo')}
    del _L0_xattn_all

    def _L0_ffn_setup():
        import jax, jax.numpy as jnp
        import numpy as np
        D_MODEL = 128
        FFN = 128
        N_EXPERTS = 8
        N_SHARED = 1
        TOP_K = 2
        B, S = (2, 256)

        def _swiglu(h):
            a, b = jnp.split(h, 2, axis=-1)
            return jax.nn.silu(a) * b
        key = jax.random.key(seed)
        ks = jax.random.split(key, 12)
        sc = 0.02
        return {'x': jax.random.normal(ks[0], (B, S, D_MODEL), dtype=jnp.float32), 'gate_w': jax.random.normal(ks[1], (D_MODEL, N_EXPERTS), dtype=jnp.float32) * sc, 'gate_b': jnp.zeros((N_EXPERTS,), dtype=jnp.float32), 'sw1': jax.random.normal(ks[2], (N_SHARED, D_MODEL, 2 * FFN), dtype=jnp.float32) * sc, 'sb1': jnp.zeros((N_SHARED, 2 * FFN), dtype=jnp.float32), 'sw2': jax.random.normal(ks[3], (N_SHARED, FFN, D_MODEL), dtype=jnp.float32) * sc, 'sb2': jnp.zeros((N_SHARED, D_MODEL), dtype=jnp.float32), 'rw1': jax.random.normal(ks[4], (N_EXPERTS, D_MODEL, 2 * FFN), dtype=jnp.float32) * sc, 'rb1': jnp.zeros((N_EXPERTS, 2 * FFN), dtype=jnp.float32), 'rw2': jax.random.normal(ks[5], (N_EXPERTS, FFN, D_MODEL), dtype=jnp.float32) * sc, 'rb2': jnp.zeros((N_EXPERTS, D_MODEL), dtype=jnp.float32)}
    _L0_ffn_all = _L0_ffn_setup()
    _L0_ffn_in = {k: v for k, v in _L0_ffn_all.items() if k in ('gate_w', 'gate_b', 'sw1', 'sb1', 'sw2', 'sb2', 'rw1', 'rb1', 'rw2', 'rb2')}
    del _L0_ffn_all
    return {'x': x, 'ctx_768': ctx_768, 'L0_xattn_Wq': _L0_xattn_in['Wq'], 'L0_xattn_Wk': _L0_xattn_in['Wk'], 'L0_xattn_Wv': _L0_xattn_in['Wv'], 'L0_xattn_Wo': _L0_xattn_in['Wo'], 'L0_ffn_gate_w': _L0_ffn_in['gate_w'], 'L0_ffn_gate_b': _L0_ffn_in['gate_b'], 'L0_ffn_sw1': _L0_ffn_in['sw1'], 'L0_ffn_sb1': _L0_ffn_in['sb1'], 'L0_ffn_sw2': _L0_ffn_in['sw2'], 'L0_ffn_sb2': _L0_ffn_in['sb2'], 'L0_ffn_rw1': _L0_ffn_in['rw1'], 'L0_ffn_rb1': _L0_ffn_in['rb1'], 'L0_ffn_rw2': _L0_ffn_in['rw2'], 'L0_ffn_rb2': _L0_ffn_in['rb2']}

def reference(x, ctx_768, L0_xattn_Wq, L0_xattn_Wk, L0_xattn_Wv, L0_xattn_Wo, L0_ffn_gate_w, L0_ffn_gate_b, L0_ffn_sw1, L0_ffn_sb1, L0_ffn_sw2, L0_ffn_sb2, L0_ffn_rw1, L0_ffn_rb1, L0_ffn_rw2, L0_ffn_rb2):
    import jax
    import jax.numpy as jnp

    def _L0_xattn_ref(q, k, Wq, Wk, Wv, Wo):
        import jax, jax.numpy as jnp
        import numpy as np
        EPS = 1e-05
        query = q @ Wq.T
        key_p = k @ Wk.T
        value = k @ Wv.T
        sim = jnp.einsum('bqd,bkd->bqk', query, key_p)
        mean = jnp.mean(sim, axis=(1, 2), keepdims=True)
        var = jnp.var(sim, axis=(1, 2), keepdims=True)
        sim = (sim - mean) * jax.lax.rsqrt(var + EPS)
        attn = jax.nn.softmax(sim, axis=-1)
        out = jnp.einsum('bqk,bkd->bqd', attn, value)
        return out @ Wo.T

    def _L0_ffn_ref(x, gate_w, gate_b, sw1, sb1, sw2, sb2, rw1, rb1, rw2, rb2):
        import jax, jax.numpy as jnp
        import numpy as np
        D_MODEL = 128
        FFN = 128
        N_EXPERTS = 8
        N_SHARED = 1
        TOP_K = 2
        B, S = (2, 256)

        def _swiglu(h):
            a, b = jnp.split(h, 2, axis=-1)
            return jax.nn.silu(a) * b
        hs = jnp.einsum('bsd,ndf->nbsf', x, sw1) + sb1[:, None, None, :]
        shared_out = jnp.einsum('nbsf,nfd->bsd', _swiglu(hs), sw2) + sb2.sum(0)
        probs = jax.nn.softmax(x @ gate_w + gate_b, axis=-1)
        topk_probs, topk_idx = jax.lax.top_k(probs, TOP_K)
        cw = jnp.sum(jax.nn.one_hot(topk_idx, N_EXPERTS, dtype=x.dtype) * topk_probs[..., None], axis=2)
        hr = jnp.einsum('bsd,edf->ebsf', x, rw1) + rb1[:, None, None, :]
        out_e = jnp.einsum('ebsf,efd->ebsd', _swiglu(hr), rw2) + rb2[:, None, None, :]
        routed_out = jnp.einsum('ebsd,bse->bsd', out_e, cw)
        return shared_out + routed_out
    x = x + _L0_xattn_ref(_layernorm(x, axis=-1), ctx_768, L0_xattn_Wq, L0_xattn_Wk, L0_xattn_Wv, L0_xattn_Wo)
    x = x + _L0_ffn_ref(_layernorm(x, axis=-1), L0_ffn_gate_w, L0_ffn_gate_b, L0_ffn_sw1, L0_ffn_sb1, L0_ffn_sw2, L0_ffn_sb2, L0_ffn_rw1, L0_ffn_rb1, L0_ffn_rw2, L0_ffn_rb2)
    return x

_drawn_inputs = setup_inputs


def setup_inputs(seed=0):
    import zlib

    import numpy as np

    out = dict(_drawn_inputs(seed))
    spreads = {'L0_ffn_gate_b': (0.0, 0.561),
     'L0_ffn_sb1': (0.0, 0.8),
     'L0_ffn_sb2': (0.0, 0.381),
     'L0_ffn_rb1': (0.0, 0.8),
     'L0_ffn_rb2': (0.0, 0.365)}
    factors = {'L0_ffn_gate_w': 3.262,
     'L0_ffn_sw1': 8.0,
     'L0_ffn_sw2': 8.0,
     'L0_ffn_rw1': 8.0,
     'L0_ffn_rw2': 8.0}
    for name, (base, spread) in spreads.items():
        noise = np.random.default_rng([zlib.crc32(name.encode()), seed]).standard_normal(out[name].shape)
        drawn = base * np.exp(spread * noise) if base else spread * noise
        out[name] = jnp.asarray(drawn.astype(out[name].dtype))
    for name, factor in factors.items():
        out[name] = (out[name] * factor).astype(out[name].dtype)
    return out
```

```python
from contextlib import ExitStack

import concourse.bass as bass
from concourse import mybir

F32 = mybir.dt.float32
F32R = mybir.dt.float32r
ALU = mybir.AluOpType
ACT = mybir.ActivationFunctionType
X = mybir.AxisListType.X

P = 128
EPS = 1e-5


def xattn_moe_kernel(nc, x, ctx, wq, wk, wv, wo, gate_w, gate_b, sw1, sb1, sw2, sb2, rw1, rb1, rw2, rb2, out):
    B, S, D = x.shape
    DC = ctx.shape[2]
    E = rw1.shape[0]
    NX = E + 1
    FF = rw2.shape[1]
    IB = S // P
    CB = 2
    TC = CB * IB
    N = TC * P
    C = B // CB
    assert D == P and FF == P and N == 512 and NX % 3 == 0

    with ExitStack() as stack:
        def sb(name, shape, dt=F32):
            return stack.enter_context(nc.sbuf_tensor(name, shape, dt))

        def sem(name):
            return stack.enter_context(nc.semaphore(name))

        bank = [stack.enter_context(nc.psum_tensor(f"bank{i}", [P, 512], F32)) for i in range(8)]

        x_sb = sb("x_sb", [P, B * IB, D])
        ctx_sb = sb("ctx_sb", [P, B * IB, DC])
        wq_sb, wk_sb, wv_sb, wo_sb = sb("wq_sb", [P, D]), sb("wk_sb", [P, DC]), sb("wv_sb", [P, DC]), sb("wo_sb", [P, D])
        w1_sb = sb("w1_sb", [P, NX, 2 * FF])
        w2_sb = sb("w2_sb", [P, NX, D])
        b1_rows = sb("b1_rows", [NX, 2 * FF])
        b2_rows = sb("b2_rows", [P, D])
        sb2_col = sb("sb2_col", [P, 1])
        gate_w_sb = sb("gate_w_sb", [P, P])
        gate_b_col = sb("gate_b_col", [P, 1])

        ident = sb("ident", [P, P])
        mean_of_partitions = sb("mean_of_partitions", [P, P])
        minus_half = sb("minus_half", [P, 8])
        descending = sb("descending", [P, E])
        pick_f = sb("pick_f", [P, E, P])
        pick = sb("pick", [P, E, P], F32R)

        wo_t = sb("wo_t", [P, D])
        qk_w = sb("qk_w", [P, DC])
        vo_w = sb("vo_w", [DC, D])
        b1_cols = sb("b1_cols", [P, 2, NX])
        w1_head, w1_rest = sb("w1_head", [P, NX, 2 * FF], F32R), sb("w1_rest", [P, NX, 2 * FF], F32R)
        w2_head, w2_rest = sb("w2_head", [P, NX, D], F32R), sb("w2_rest", [P, NX, D], F32R)
        b2_head, b2_rest = sb("b2_head", [P, D], F32R), sb("b2_rest", [P, D], F32R)
        gate_head, gate_rest = sb("gate_head", [P, P], F32R), sb("gate_rest", [P, P], F32R)

        ln_stats = sb("ln_stats", [P, 2, TC, 6])
        ln_mv = sb("ln_mv", [P, 2, TC, 2])
        ln_veps = sb("ln_veps", [P, 2, TC])
        ln_rstd = sb("ln_rstd", [P, 2, TC])
        xn = sb("xn", [P, 2, TC, D])
        xn_t = sb("xn_t", [P, N])
        ctx_t = sb("ctx_t", [DC, N])
        t_sb = sb("t_sb", [DC, N])
        v_sb = sb("v_sb", [P, C, TC, D])
        row_max = sb("row_max", [P, CB, IB])
        sim_stats = sb("sim_stats", [P, CB, 6])
        sim_mv = sb("sim_mv", [P, CB, 2])
        sim_avg = sb("sim_avg", [P, CB, 2])
        sim_nvar = sb("sim_nvar", [P, CB])
        sim_veps = sb("sim_veps", [P, CB])
        sim_r = sb("sim_r", [P, CB])
        neg_max = sb("neg_max", [P, CB, IB])
        prob = sb("prob", [P, CB, IB, S])
        row_sum = sb("row_sum", [P, CB, IB])
        row_inv = sb("row_inv", [P, CB, IB])
        prob_t = sb("prob_t", [P, CB, IB, S])
        x1 = sb("x1", [P, B * IB, D])

        logits_t = sb("logits_t", [E, N])
        logits = sb("logits", [P, TC, E])
        g_max, g_sum, g_inv = sb("g_max", [P, TC]), sb("g_sum", [P, TC]), sb("g_inv", [P, TC])
        g_z, g_exp, g_p = sb("g_z", [P, TC, E]), sb("g_exp", [P, TC, E]), sb("g_p", [P, TC, E])
        g_best = [sb(f"g_best{k}", [P, TC]) for k in range(2)]
        g_first = [sb(f"g_first{k}", [P, TC]) for k in range(2)]
        g_eq = [sb(f"g_eq{k}", [P, TC, E]) for k in range(2)]
        g_rank = [sb(f"g_rank{k}", [P, TC, E]) for k in range(2)]
        g_hot = [sb(f"g_hot{k}", [P, TC, E]) for k in range(2)]
        g_left, g_mask, g_cw = sb("g_left", [P, TC, E]), sb("g_mask", [P, TC, E]), sb("g_cw", [P, TC, E])
        cw_parts = sb("cw_parts", [P, TC, 2, E])
        cw_head = sb("cw_head", [P, TC, E], F32R)

        x2_head = sb("x2_head", [P, C, N], F32R)
        x2_rest = sb("x2_rest", [P, C, N], F32R)
        cw_t = sb("cw_t", [P, C, N], F32R)
        silu = sb("silu", [P, 3, N])
        act = sb("act", [P, 3, N])
        act_head = sb("act_head", [P, 3, N], F32R)
        act_rest = sb("act_rest", [P, 3, N], F32R)
        out_t = sb("out_t", [P, N])

        x_in = [sem(f"x_in{c}") for c in range(C)]
        ctx_in = [sem(f"ctx_in{c}") for c in range(C)]
        attn_w_in, ffn_w_in, small_in, stored = sem("attn_w_in"), sem("ffn_w_in"), sem("small_in"), sem("stored")
        ident_ready, consts_ready, pool_order, w_split = sem("ident_ready"), sem("consts_ready"), sem("pool_order"), sem("w_split")
        setup_ps, setup_sb = sem("setup_ps"), sem("setup_sb")
        dve_order = sem("dve_order")
        ln_var, ln_r, xn_ready = [sem("ln1_var"), sem("ln2_var")], [sem("ln1_r"), sem("ln2_r")], [sem("xn1_ready"), sem("xn2_ready")]
        xnt_ps, xnt_sb, ctxt_ps, ctxt_sb = sem("xnt_ps"), sem("xnt_sb"), sem("ctxt_ps"), sem("ctxt_sb")
        t_ps, t_ready, v_ps, v_ready = sem("t_ps"), sem("t_ready"), sem("v_ps"), sem("v_ready")
        sim_ps, simstat_sb, simavg_ps, simavg_sb = sem("sim_ps"), sem("simstat_sb"), sem("simavg_ps"), sem("simavg_sb")
        simvar_sb, simr_sb, negmax_sb = sem("simvar_sb"), sem("simr_sb"), sem("negmax_sb")
        prob_sb, probt_ps, probt_sb, attn_ps, x1_ready = sem("prob_sb"), sem("probt_ps"), sem("probt_sb"), sem("attn_ps"), sem("x1_ready")
        x2t_ps, x2_head_sb, x2_rest_sb = sem("x2t_ps"), sem("x2_head_sb"), sem("x2_rest_sb")
        lgt_ps, lgt_sb, lg_ps, lg_sb = sem("lgt_ps"), sem("lgt_sb"), sem("lg_ps"), sem("lg_sb")
        gz_sb, gexp_sb, cw_sb, cwt_ps, cwt_sb = sem("gz_sb"), sem("gexp_sb"), sem("cw_sb"), sem("cwt_ps"), sem("cwt_sb")
        a_ps, b_ps, cw_ps, silu_sb, scaled_sb = sem("a_ps"), sem("b_ps"), sem("cw_ps"), sem("silu_sb"), sem("scaled_sb")
        act_sb, head_sb, rest_sb, y_ps = sem("act_sb"), sem("head_sb"), sem("rest_sb"), sem("y_ps")
        out_ps, outt_sb, tok_ps, final_sb = sem("out_ps"), sem("outt_sb"), sem("tok_ps"), sem("final_sb")

        x_dram = x.rearrange("b (p i) d -> p b i d", i=IB)
        ctx_dram = ctx.rearrange("b (p i) d -> p b i d", i=IB)
        out_dram = out.rearrange("(c b) (p i) d -> c p b (i d)", i=IB, b=CB)

        def tiles(c):
            return slice(TC * c, TC * (c + 1))

        def per_token(v, shape):
            return v.unsqueeze(2).broadcast_to(shape)

        XT, CT, SIM, PT, AVG, X2 = bank[0], bank[1], bank[2:4], bank[4:6], bank[6], bank[7]
        A_B, B_B, CW_B, OUT_B = bank[0:3], bank[3:6], bank[6], bank[7]

        block = stack.enter_context(nc.Block())

        @block.sync
        def _(sp):
            def load_x(c):
                sp.dma_start(x_sb[:, tiles(c), :].rearrange("p (b i) d -> p b i d", i=IB),
                             x_dram[:, CB * c:CB * (c + 1)]).then_inc(x_in[c], 16)

            def load_ctx(c):
                sp.dma_start(ctx_sb[:, tiles(c), :].rearrange("p (b i) d -> p b i d", i=IB),
                             ctx_dram[:, CB * c:CB * (c + 1)]).then_inc(ctx_in[c], 16)

            load_x(0)
            for dst, src in ((wq_sb, wq), (wk_sb, wk), (wo_sb, wo), (wv_sb, wv)):
                sp.dma_start(dst[:, :], src).then_inc(attn_w_in, 16)
            load_ctx(0)
            load_x(1)
            load_ctx(1)
            sp.dma_start(b1_rows[0:1, :], sb1).then_inc(small_in, 16)
            sp.dma_start(b1_rows[1:NX, :], rb1).then_inc(small_in, 16)
            sp.dma_start(sb2_col[:, :], sb2.rearrange("a d -> d a")).then_inc(small_in, 16)
            sp.dma_start(gate_b_col[0:E, :], gate_b.rearrange("(e a) -> e a", a=1)).then_inc(small_in, 16)
            sp.wait_ge(consts_ready, 1)
            sp.dma_start(b2_rows[0:E, :], rb2).then_inc(small_in, 16)
            sp.dma_start(b2_rows[E:2 * E, :], rb2).then_inc(small_in, 16)
            sp.dma_start(gate_w_sb[:, 0:E], gate_w).then_inc(small_in, 16)
            for c in range(2, C):
                load_x(c)
                load_ctx(c)
            sp.dma_start(w1_sb[:, 0, :], sw1[0]).then_inc(ffn_w_in, 16)
            sp.dma_start(w1_sb[:, 1:NX, :], rw1.rearrange("e d f -> d e f")).then_inc(ffn_w_in, 16)
            sp.dma_start(w2_sb[:, 0, :], sw2[0]).then_inc(ffn_w_in, 16)
            sp.dma_start(w2_sb[:, 1:NX, :], rw2.rearrange("e f d -> f e d")).then_inc(ffn_w_in, 16)
            for c in range(C):
                sp.wait_ge(final_sb, c + 1)
                sp.dma_start(out_dram[c], x1[:, tiles(c), :].rearrange("p (b i) d -> p b (i d)", i=IB)).then_inc(stored, 16)
            sp.wait_ge(stored, 16 * C)

        @block.gpsimd
        def _(pool):
            order = [0]

            def wait_own(ins):
                order[0] += 1
                ins.then_inc(pool_order, 1)
                pool.wait_ge(pool_order, order[0])

            wait_own(pool.memset(ident[:, :], 0.0))
            pool.affine_select(out=ident[:, :], in_=ident[:, :], compare_op=ALU.not_equal, fill=1.0, base=0,
                               pattern=[[-1, P]], channel_multiplier=1).then_inc(ident_ready, 1)
            wait_own(pool.memset(minus_half[:, :], -0.5))

            def rstd(which, c):
                pool.wait_ge(ln_var[which], c + 1)
                if c >= 1:
                    pool.wait_ge(xn_ready[which], c)
                pool.tensor_tensor(ln_rstd[:, which, :], ln_veps[:, which, :], minus_half[:, 0:TC], ALU.pow).then_inc(ln_r[which], 1)

            def sim_rstd(m):
                j = m % CB
                pool.wait_ge(simvar_sb, m + 1)
                if m >= CB:
                    pool.wait_ge(prob_sb, m - CB + 1)
                pool.tensor_tensor(sim_r[:, j:j + 1], sim_veps[:, j:j + 1], minus_half[:, 0:1], ALU.pow).then_inc(simr_sb, 1)

            def split(head, rest, whole):
                pool.tensor_copy(head, whole).then_inc(w_split, 1)
                order[0] += 0
                splits[0] += 1
                pool.wait_ge(w_split, splits[0])
                pool.tensor_tensor(rest, whole, head.bitcast(F32), ALU.subtract).then_inc(w_split, 1)
                splits[0] += 1

            splits = [0]
            wait_own(pool.memset(gate_w_sb[:, :], 0.0))
            wait_own(pool.memset(b2_rows[:, :], 0.0))
            pool.memset(mean_of_partitions[:, :], 1.0 / P).then_inc(consts_ready, 1)
            for k in range(E):
                pool.memset(descending[:, k:k + 1], float(E - k)).then_inc(consts_ready, 1)
            pool.memset(cw_t[:, :, :].bitcast(F32), 0.0).then_inc(consts_ready, 1)
            rstd(0, 0)
            wait_own(pool.memset(pick_f[:, :, :], 0.0))
            for base in (0, -E):
                wait_own(pool.affine_select(out=pick_f[:, :, :], in_=pick_f[:, :, :], compare_op=ALU.not_equal, fill=1.0,
                                            base=base, pattern=[[-1, E], [0, P]], channel_multiplier=1))
            pool.tensor_copy(pick[:, :, :], pick_f[:, :, :]).then_inc(consts_ready, 1)
            rstd(0, 1)
            pool.wait_ge(small_in, 16 * 7)
            split(gate_head[:, :], gate_rest[:, :], gate_w_sb[:, :])
            split(b2_head[:, :], b2_rest[:, :], b2_rows[:, :])
            for c in range(C):
                for j in range(CB):
                    sim_rstd(CB * c + j)
                if c + 2 < C:
                    rstd(0, c + 2)
                if c == 0:
                    pool.wait_ge(ffn_w_in, 64)
                lo, hi = NX * c // C, NX * (c + 1) // C
                if c < C - 1:
                    split(w1_head[:, lo:hi, :], w1_rest[:, lo:hi, :], w1_sb[:, lo:hi, :])
                    split(w2_head[:, lo:hi, :], w2_rest[:, lo:hi, :], w2_sb[:, lo:hi, :])
                rstd(1, c)
                if c == C - 1:
                    split(w1_head[:, lo:hi, :], w1_rest[:, lo:hi, :], w1_sb[:, lo:hi, :])
                    split(w2_head[:, lo:hi, :], w2_rest[:, lo:hi, :], w2_sb[:, lo:hi, :])

            def expert_rest(c, e, first):
                n, k = NX * c + e, e % 3
                pool.wait_ge(head_sb, n + 1)
                if not first or e >= 3:
                    pool.wait_ge(y_ps, n - 2)
                pool.tensor_tensor(act_rest[:, k, :], act[:, k, :], act_head[:, k, :].bitcast(F32), ALU.subtract).then_inc(rest_sb, 1)

            for e in range(NX):
                expert_rest(0, e, True)
            with pool.Fori(1, C) as c:
                for e in range(NX):
                    expert_rest(c, e, False)

        @block.scalar
        def _(act_eng):
            copy = act_eng.copy

            act_eng.wait_ge(setup_ps, 1)
            copy(wo_t[:, :], bank[0][:, 0:D]).then_inc(setup_sb, 1)
            act_eng.wait_ge(setup_ps, 2)
            copy(qk_w[:, :], bank[1][:, 0:DC]).then_inc(setup_sb, 1)

            def xnt(c):
                act_eng.wait_ge(xnt_ps, c + 1)
                if c >= 1:
                    act_eng.wait_ge(t_ps, c)
                copy(xn_t[:, :], XT[:, :]).then_inc(xnt_sb, 1)

            def ctxt(c):
                act_eng.wait_ge(ctxt_ps, c + 1)
                if c >= 1:
                    act_eng.wait_ge(sim_ps, CB * c)
                copy(ctx_t[:, :], CT[0:DC, :]).then_inc(ctxt_sb, 1)

            def t_copy(c):
                act_eng.wait_ge(t_ps, c + 1)
                if c >= 1:
                    act_eng.wait_ge(sim_ps, CB * c)
                copy(t_sb[:, :], XT[0:DC, :]).then_inc(t_ready, 1)

            def v_copy(c):
                act_eng.wait_ge(v_ps, c + 1)
                copy(v_sb[:, c].rearrange("p t d -> p (t d)"), CT[:, :]).then_inc(v_ready, 1)

            def exponentials(m):
                j = m % CB
                act_eng.wait_ge(negmax_sb, m + 1)
                if m >= CB:
                    act_eng.wait_ge(probt_ps, m - CB + 1)
                    act_eng.wait_ge(x1_ready, m - CB + 1)
                for i in range(IB):
                    last = act_eng.activation(prob[:, j, i, :], SIM[j][:, i * S:(i + 1) * S], ACT.Exp,
                                              bias=neg_max[:, j, i:i + 1], scale=sim_r[:, j:j + 1],
                                              accum_out=row_sum[:, j, i:i + 1])
                last.then_inc(prob_sb, 1)

            def probt(m):
                j = m % CB
                act_eng.wait_ge(probt_ps, m + 1)
                if m >= CB:
                    act_eng.wait_ge(attn_ps, m - CB + 1)
                copy(prob_t[:, j].rearrange("p k q -> p (k q)"), PT[j][:, :]).then_inc(probt_sb, 1)

            def x2_heads(c):
                act_eng.wait_ge(x2t_ps, c + 1)
                copy(x2_head[:, c, :], X2[:, :]).then_inc(x2_head_sb, 1)

            def logits_bias(c):
                act_eng.wait_ge(lgt_ps, c + 1)
                if c >= 1:
                    act_eng.wait_ge(lg_ps, c)
                act_eng.activation(logits_t[:, :], X2[0:E, :], ACT.Identity, bias=gate_b_col[0:E, :]).then_inc(lgt_sb, 1)

            def logits_copy(c):
                act_eng.wait_ge(lg_ps, c + 1)
                if c >= 1:
                    act_eng.wait_ge(gz_sb, c)
                copy(logits[:, :, :].rearrange("p t e -> p (t e)"), X2[:, 0:TC * E]).then_inc(lg_sb, 1)

            def gate_exp(c):
                act_eng.wait_ge(gz_sb, c + 1)
                if c >= 1:
                    act_eng.wait_ge(cw_sb, c)
                act_eng.activation(g_exp[:, :, :], g_z[:, :, :], ACT.Exp).then_inc(gexp_sb, 1)

            def cwt(c):
                act_eng.wait_ge(cwt_ps, c + 1)
                if c == 0:
                    act_eng.wait_ge(consts_ready, 2 + E)
                copy(cw_t[0:2 * E, c, :], X2[0:2 * E, :]).then_inc(cwt_sb, 1)

            xnt(0)
            ctxt(0)
            act_eng.wait_ge(setup_ps, 3)
            copy(vo_w[:, :], bank[2][0:DC, 0:D]).then_inc(setup_sb, 1)
            t_copy(0)
            v_copy(0)
            act_eng.wait_ge(setup_ps, 4)
            copy(b1_cols[:, :, :].rearrange("p h e -> p (h e)"), bank[7][:, 0:2 * NX]).then_inc(setup_sb, 1)
            act_eng.wait_ge(small_in, 16 * 7)
            for c in range(C + 1):
                if c + 1 < C:
                    xnt(c + 1)
                    ctxt(c + 1)
                if c >= 1:
                    x2_heads(c - 1)
                if c + 1 < C:
                    t_copy(c + 1)
                    v_copy(c + 1)
                if c < C:
                    exponentials(CB * c)
                    exponentials(CB * c + 1)
                if c >= 1:
                    logits_bias(c - 1)
                if c < C:
                    probt(CB * c)
                    probt(CB * c + 1)
                if c >= 1:
                    logits_copy(c - 1)
                    gate_exp(c - 1)
                    cwt(c - 1)

            def expert_silu(c, e, first):
                n, k = NX * c + e, e % 3
                act_eng.wait_ge(a_ps, n + 1)
                if not first or e >= 3:
                    act_eng.wait_ge(act_sb, n - 2)
                act_eng.activation(silu[:, k, :], A_B[k][:, :], ACT.Silu, bias=b1_cols[:, 0, e:e + 1]).then_inc(silu_sb, 1)

            def expert_head(c, e, first):
                n, k = NX * c + e, e % 3
                act_eng.wait_ge(act_sb, n + 1)
                if not first or e >= 3:
                    act_eng.wait_ge(y_ps, n - 2)
                copy(act_head[:, k, :], act[:, k, :]).then_inc(head_sb, 1)

            def out_bias(c):
                act_eng.wait_ge(out_ps, c + 1)
                act_eng.activation(out_t[:, :], OUT_B[:, :], ACT.Identity, bias=sb2_col[:, :]).then_inc(outt_sb, 1)

            def expert_chunk(c, first):
                for e in range(NX):
                    expert_silu(c, e, first)
                    if e >= 1:
                        expert_head(c, e - 1, first)
                    elif not first:
                        expert_head(c - 1, NX - 1, False)
                    if e == 2 and not first:
                        out_bias(c - 1)

            expert_chunk(0, True)
            with act_eng.Fori(1, C) as c:
                expert_chunk(c, False)
            expert_head(C - 1, NX - 1, False)
            out_bias(C - 1)

        @block.vector
        def _(dve):
            order = [0]

            def own(ins):
                order[0] += 1
                return ins.then_inc(dve_order, 1)

            def wait_own():
                dve.wait_ge(dve_order, order[0])

            def ln_statistics(which, c, src):
                for i in range(TC):
                    own(dve.bn_stats(ln_stats[:, which, i, :], src[:, TC * c + i, :]))
                wait_own()
                for i in range(TC):
                    own(dve.bn_aggr(ln_mv[:, which, i, :], ln_stats[:, which, i, :]))
                wait_own()
                if c >= 1:
                    dve.wait_ge(ln_r[which], c)
                dve.tensor_scalar(ln_veps[:, which, :], ln_mv[:, which, :, 1], EPS, None, ALU.add).then_inc(ln_var[which], 1)

            def ln_normalise(which, c, src, transposed):
                dve.wait_ge(ln_r[which], c + 1)
                if c >= 1:
                    dve.wait_ge(transposed, c)
                for i in range(TC):
                    last = dve.tensor_scalar(xn[:, which, i, :], src[:, TC * c + i, :], ln_mv[:, which, i, 0:1],
                                             ln_rstd[:, which, i:i + 1], ALU.subtract, ALU.mult)
                last.then_inc(xn_ready[which], 1)

            def scores_statistics(m):
                j = m % CB
                dve.wait_ge(sim_ps, m + 1)
                own(dve.tensor_reduce(row_max[:, j, :], SIM[j][:, :].rearrange("p (i k) -> p i k", i=IB), X, ALU.max))
                own(dve.bn_stats(sim_stats[:, j, :], SIM[j][:, :]))
                wait_own()
                own(dve.bn_aggr(sim_mv[:, j, :], sim_stats[:, j, :]))
                wait_own()
                dve.scalar_tensor_tensor(sim_mv[:, j, 1:2], sim_mv[:, j, 0:1], sim_mv[:, j, 0:1], sim_mv[:, j, 1:2],
                                         ALU.mult, ALU.add).then_inc(simstat_sb, 1)

            def scores_variance(m):
                j = m % CB
                dve.wait_ge(simavg_ps, m + 1)
                dve.tensor_copy(sim_avg[:, j, :], AVG[:, 0:2]).then_inc(simavg_sb, 1)
                dve.wait_ge(simavg_sb, m + 1)
                own(dve.scalar_tensor_tensor(sim_nvar[:, j:j + 1], sim_avg[:, j, 0:1], sim_avg[:, j, 0:1], sim_avg[:, j, 1:2],
                                             ALU.mult, ALU.subtract))
                wait_own()
                dve.tensor_scalar(sim_veps[:, j:j + 1], sim_nvar[:, j:j + 1], -1.0, EPS, ALU.mult, ALU.add).then_inc(simvar_sb, 1)

            def scores_scale(m):
                j = m % CB
                dve.wait_ge(simr_sb, m + 1)
                dve.tensor_scalar(neg_max[:, j, :], row_max[:, j, :], sim_r[:, j:j + 1], -1.0, ALU.mult, ALU.mult).then_inc(negmax_sb, 1)

            def residual(m):
                j, t = m % CB, IB * m
                dve.wait_ge(prob_sb, m + 1)
                own(dve.reciprocal(row_inv[:, j, :], row_sum[:, j, :]))
                wait_own()
                dve.wait_ge(attn_ps, m + 1)
                for i in range(IB):
                    last = dve.scalar_tensor_tensor(x1[:, t + i, :], SIM[j][:, i * D:(i + 1) * D], row_inv[:, j, i:i + 1],
                                                    x_sb[:, t + i, :], ALU.mult, ALU.add)
                last.then_inc(x1_ready, 1)

            def x2_rests(c):
                dve.wait_ge(x2_head_sb, c + 1)
                dve.tensor_tensor(x2_rest[:, c, :], X2[:, :], x2_head[:, c, :].bitcast(F32), ALU.subtract).then_inc(x2_rest_sb, 1)

            full = [P, TC, E]

            def router_logits(c):
                dve.wait_ge(lg_sb, c + 1)
                own(dve.tensor_reduce(g_max[:, :], logits[:, :, :], X, ALU.max))
                wait_own()
                if c >= 1:
                    dve.wait_ge(gexp_sb, c)
                dve.tensor_tensor(g_z[:, :, :], logits[:, :, :], per_token(g_max[:, :], full), ALU.subtract).then_inc(gz_sb, 1)

            def router_weights(c):
                dve.wait_ge(gexp_sb, c + 1)
                own(dve.tensor_reduce(g_sum[:, :], g_exp[:, :, :], X, ALU.add))
                wait_own()
                own(dve.reciprocal(g_inv[:, :], g_sum[:, :]))
                wait_own()
                own(dve.tensor_tensor(g_p[:, :, :], g_exp[:, :, :], per_token(g_inv[:, :], full), ALU.mult))
                wait_own()
                left = g_p
                for k in range(2):
                    own(dve.tensor_reduce(g_best[k][:, :], left[:, :, :], X, ALU.max))
                    wait_own()
                    own(dve.tensor_tensor(g_eq[k][:, :, :], left[:, :, :], per_token(g_best[k][:, :], full), ALU.is_ge))
                    wait_own()
                    own(dve.tensor_tensor(g_rank[k][:, :, :], g_eq[k][:, :, :],
                                          descending[:, :].unsqueeze(1).broadcast_to(full), ALU.mult))
                    wait_own()
                    own(dve.tensor_reduce(g_first[k][:, :], g_rank[k][:, :, :], X, ALU.max))
                    wait_own()
                    own(dve.tensor_tensor(g_hot[k][:, :, :], g_rank[k][:, :, :], per_token(g_first[k][:, :], full), ALU.is_equal))
                    wait_own()
                    if k == 0:
                        own(dve.scalar_tensor_tensor(g_left[:, :, :], g_hot[0][:, :, :], -2.0, g_p[:, :, :], ALU.mult, ALU.add))
                        wait_own()
                        left = g_left
                own(dve.tensor_tensor(g_mask[:, :, :], g_hot[0][:, :, :], g_hot[1][:, :, :], ALU.add))
                wait_own()
                own(dve.tensor_tensor(g_cw[:, :, :], g_mask[:, :, :], g_p[:, :, :], ALU.mult))
                wait_own()
                own(dve.tensor_copy(cw_head[:, :, :], g_cw[:, :, :]))
                wait_own()
                if c >= 1:
                    dve.wait_ge(cwt_ps, c)
                own(dve.tensor_copy(cw_parts[:, :, 0, :], cw_head[:, :, :].bitcast(F32)))
                own(dve.tensor_tensor(cw_parts[:, :, 1, :], g_cw[:, :, :], cw_head[:, :, :].bitcast(F32), ALU.subtract))
                wait_own()
                dve.sem_inc(cw_sb, 1)

            for c in range(2):
                dve.wait_ge(x_in[c], 16)
                ln_statistics(0, c, x_sb)
                ln_normalise(0, c, x_sb, xnt_ps)
            dve.wait_ge(consts_ready, 1 + E)
            for c in range(C + 1):
                if c < C:
                    for j in range(CB):
                        scores_statistics(CB * c + j)
                if c < C:
                    for j in range(CB):
                        scores_variance(CB * c + j)
                if c >= 1:
                    x2_rests(c - 1)
                if c < C:
                    for j in range(CB):
                        scores_scale(CB * c + j)
                if c + 2 < C:
                    dve.wait_ge(x_in[c + 2], 16)
                    ln_statistics(0, c + 2, x_sb)
                    ln_normalise(0, c + 2, x_sb, xnt_ps)
                if c >= 1:
                    router_logits(c - 1)
                    router_weights(c - 1)
                if c < C:
                    for j in range(CB):
                        residual(CB * c + j)
                    dve.wait_ge(x1_ready, CB * (c + 1))
                    ln_statistics(1, c, x1)
                    ln_normalise(1, c, x1, x2t_ps)

            def expert_gate(c, e, first):
                n, k = NX * c + e, e % 3
                dve.wait_ge(silu_sb, n + 1)
                if e >= 1:
                    dve.wait_ge(cw_ps, E * c + e)
                    dve.tensor_tensor(silu[:, k, :], silu[:, k, :], CW_B[:, :], ALU.mult).then_inc(scaled_sb, 1)
                    dve.wait_ge(scaled_sb, E * c + e)
                dve.wait_ge(b_ps, n + 1)
                if not first or e >= 3:
                    dve.wait_ge(rest_sb, n - 2)
                dve.scalar_tensor_tensor(act[:, k, :], B_B[k][:, :], b1_cols[:, 1, e:e + 1], silu[:, k, :],
                                         ALU.add, ALU.mult).then_inc(act_sb, 1)

            def final(c):
                dve.wait_ge(tok_ps, c + 1)
                rows = x1[:, bass.ds(TC * c, TC), :]
                dve.tensor_tensor(rows, CW_B[:, :].rearrange("p (t d) -> p t d", t=TC), rows, ALU.add).then_inc(final_sb, 1)

            def expert_chunk(c, first):
                for e in range(NX):
                    if e == 3 and not first:
                        final(c - 1)
                    expert_gate(c, e, first)

            dve.wait_ge(setup_sb, 4)
            expert_chunk(0, True)
            with dve.Fori(1, C) as c:
                expert_chunk(c, False)
            final(C - 1)

        @block.tensor
        def _(pe):
            def mm(dst, lhs, rhs, start=True, stop=True):
                return pe.matmul(dst, lhs, rhs, start=start, stop=stop, skip_group_check=True)

            pe.wait_ge(ident_ready, 1)
            pe.wait_ge(attn_w_in, 64)
            pe.transpose(bank[0][:, 0:D], wo_sb[:, :], ident[:, :]).then_inc(setup_ps, 1)
            mm(bank[1][:, 0:DC], wq_sb[:, :], wk_sb[:, :]).then_inc(setup_ps, 1)

            def transpose_x(c):
                pe.wait_ge(xn_ready[0], c + 1)
                if c >= 1:
                    pe.wait_ge(t_ready, c)
                else:
                    pe.wait_ge(setup_sb, 1)
                for i in range(TC):
                    last = pe.transpose(XT[:, i * P:(i + 1) * P], xn[:, 0, i, :], ident[:, :])
                last.then_inc(xnt_ps, 1)

            def transpose_ctx(c):
                pe.wait_ge(ctx_in[c], 16)
                if c >= 1:
                    pe.wait_ge(v_ready, c)
                else:
                    pe.wait_ge(setup_sb, 2)
                for i in range(TC):
                    last = pe.transpose(CT[0:DC, i * P:(i + 1) * P], ctx_sb[:, TC * c + i, :], ident[:, :])
                last.then_inc(ctxt_ps, 1)

            def project_q(c):
                pe.wait_ge(xnt_sb, c + 1)
                mm(XT[0:DC, :], qk_w[:, :], xn_t[:, :]).then_inc(t_ps, 1)

            def project_v(c):
                pe.wait_ge(ctxt_sb, c + 1)
                for i in range(TC):
                    last = mm(CT[:, i * D:(i + 1) * D], ctx_t[:, i * P:(i + 1) * P], vo_w[:, :])
                last.then_inc(v_ps, 1)

            def scores(m):
                j = m % CB
                pe.wait_ge(t_ready, m // CB + 1)
                pe.wait_ge(ctxt_sb, m // CB + 1)
                if m >= CB:
                    pe.wait_ge(x1_ready, m - CB + 1)
                for i in range(IB):
                    q = (IB * j + i) * P
                    last = mm(SIM[j][:, i * S:(i + 1) * S], t_sb[:, q:q + P], ctx_t[:, j * S:(j + 1) * S])
                last.then_inc(sim_ps, 1)

            def scores_average(m):
                pe.wait_ge(simstat_sb, m + 1)
                if m == 0:
                    pe.wait_ge(consts_ready, 1)
                else:
                    pe.wait_ge(simavg_sb, m)
                mm(AVG[:, 0:2], mean_of_partitions[:, :], sim_mv[:, m % CB, :]).then_inc(simavg_ps, 1)

            def transpose_prob(m):
                j = m % CB
                pe.wait_ge(prob_sb, m + 1)
                if m >= CB:
                    pe.wait_ge(probt_sb, m - CB + 1)
                for k in range(IB):
                    for i in range(IB):
                        last = pe.transpose(PT[j][:, k * S + i * P:k * S + (i + 1) * P], prob[:, j, i, k * P:(k + 1) * P], ident[:, :])
                last.then_inc(probt_ps, 1)

            def attend(m):
                c, j = m // CB, m % CB
                pe.wait_ge(probt_sb, m + 1)
                pe.wait_ge(v_ready, c + 1)
                for i in range(IB):
                    for k in range(IB):
                        last = mm(SIM[j][:, i * D:(i + 1) * D], prob_t[:, j, k, i * P:(i + 1) * P], v_sb[:, c, IB * j + k, :],
                                  start=k == 0, stop=k == IB - 1)
                last.then_inc(attn_ps, 1)

            def transpose_x2(c):
                pe.wait_ge(xn_ready[1], c + 1)
                if c >= 1:
                    pe.wait_ge(cwt_sb, c)
                else:
                    pe.wait_ge(setup_sb, 4)
                for i in range(TC):
                    last = pe.transpose(X2[:, i * P:(i + 1) * P], xn[:, 1, i, :], ident[:, :])
                last.then_inc(x2t_ps, 1)

            def router(c):
                pe.wait_ge(x2_head_sb, c + 1)
                pe.wait_ge(x2_rest_sb, c + 1)
                if c == 0:
                    pe.wait_ge(w_split, 2)
                parts = [(g, xs) for g in (gate_head, gate_rest) for xs in (x2_head, x2_rest)]
                for k, (g, xs) in enumerate(parts):
                    last = mm(X2[:, :], g[:, :], xs[:, c, :], start=k == 0, stop=k == 3)
                last.then_inc(lgt_ps, 1)

            def transpose_logits(c):
                pe.wait_ge(lgt_sb, c + 1)
                for i in range(TC):
                    last = pe.transpose(X2[:, i * E:(i + 1) * E], logits_t[:, i * P:(i + 1) * P], ident[0:E, 0:E])
                last.then_inc(lg_ps, 1)

            def transpose_cw(c):
                pe.wait_ge(cw_sb, c + 1)
                pe.wait_ge(lg_sb, c + 1)
                for i in range(TC):
                    last = pe.transpose(X2[0:2 * E, i * P:(i + 1) * P], cw_parts[:, i].rearrange("p h e -> p (h e)"), ident[:, :])
                last.then_inc(cwt_ps, 1)

            transpose_x(0)
            transpose_ctx(0)
            mm(bank[2][0:DC, 0:D], wv_sb[:, :], wo_t[:, :]).then_inc(setup_ps, 1)
            project_q(0)
            pe.wait_ge(setup_sb, 3)
            project_v(0)
            pe.wait_ge(small_in, 16 * 7)
            for h in range(2):
                last = pe.transpose(bank[7][:, h * NX:(h + 1) * NX], b1_rows[:, h * FF:(h + 1) * FF], ident[0:NX, 0:NX])
            last.then_inc(setup_ps, 1)
            scores(0)
            scores(1)
            for c in range(C + 1):
                if c + 1 < C:
                    transpose_x(c + 1)
                    transpose_ctx(c + 1)
                if c < C:
                    scores_average(CB * c)
                    scores_average(CB * c + 1)
                if c >= 1:
                    transpose_x2(c - 1)
                if c + 1 < C:
                    project_q(c + 1)
                    project_v(c + 1)
                if c >= 1:
                    router(c - 1)
                if c < C:
                    transpose_prob(CB * c)
                    transpose_prob(CB * c + 1)
                if c >= 1:
                    transpose_logits(c - 1)
                if c < C:
                    attend(CB * c)
                    attend(CB * c + 1)
                if c + 1 < C:
                    scores(CB * (c + 1))
                    scores(CB * (c + 1) + 1)
                if c >= 1:
                    transpose_cw(c - 1)

            def hidden(c, e, half, free):
                dst = (A_B, B_B)[half][e % 3]
                cols = slice(half * FF, (half + 1) * FF)
                if free is not None:
                    pe.wait_ge(*free)
                mm(dst[:, :], w1_head[:, e, cols], x2_head[:, bass.ds(c, 1), :], True, False)
                mm(dst[:, :], w1_head[:, e, cols], x2_rest[:, bass.ds(c, 1), :], False, False)
                mm(dst[:, :], w1_rest[:, e, cols], x2_head[:, bass.ds(c, 1), :], False, True).then_inc((a_ps, b_ps)[half], 1)

            def spread_cw(c, e, first):
                if not first or e >= 2:
                    pe.wait_ge(scaled_sb, E * c + e - 1)
                if e == 3 and not first:
                    pe.wait_ge(final_sb, c)
                mm(CW_B[:, :], pick[:, e - 1, :], cw_t[:, bass.ds(c, 1), :]).then_inc(cw_ps, 1)

            def down(c, e, first):
                n, k = NX * c + e, e % 3
                pe.wait_ge(head_sb, n + 1)
                pe.wait_ge(rest_sb, n + 1)
                if e == 0 and not first:
                    pe.wait_ge(outt_sb, c)
                mm(OUT_B[:, :], w2_head[:, e, :], act_head[:, k, :], e == 0, False)
                mm(OUT_B[:, :], w2_head[:, e, :], act_rest[:, k, :], False, False)
                mm(OUT_B[:, :], w2_rest[:, e, :], act_head[:, k, :], False, e == NX - 1).then_inc(y_ps, 1)
                if e == 1:
                    mm(OUT_B[:, :], b2_head[:, :], cw_t[:, bass.ds(c, 1), :], False, False)
                    mm(OUT_B[:, :], b2_rest[:, :], cw_t[:, bass.ds(c, 1), :], False, False)

            def to_tokens(c, cw_used):
                pe.wait_ge(outt_sb, c + 1)
                pe.wait_ge(scaled_sb, cw_used)
                for i in range(TC):
                    last = pe.transpose(CW_B[:, i * P:(i + 1) * P], out_t[:, i * P:(i + 1) * P], ident[:, :])
                last.then_inc(tok_ps, 1)

            def expert_chunk(c, first):
                for e in range(NX):
                    n = NX * c + e
                    late = not first or e >= 3
                    hidden(c, e, 0, (silu_sb, n - 2) if late else None)
                    if e == 3 and not first:
                        to_tokens(c - 1, E * c + e - 1)
                    hidden(c, e, 1, (act_sb, n - 2) if late else None)
                    if e >= 1 and e != 3:
                        spread_cw(c, e, first)
                    if e >= 2:
                        down(c, e - 2, first)
                    elif not first:
                        if e == 0:
                            down(c - 1, NX - 2, False)
                        else:
                            down(c - 1, NX - 1, False)
                            pe.wait_ge(y_ps, n - 1)
                            pe.sem_inc(out_ps, 1)
                    if e == 3:
                        spread_cw(c, e, first)

            pe.wait_ge(cwt_sb, C)
            pe.wait_ge(x1_ready, B)
            pe.wait_ge(w_split, 4 + 4 * C)
            pe.wait_ge(consts_ready, 3 + E)
            expert_chunk(0, True)
            with pe.Fori(1, C) as c:
                expert_chunk(c, False)
            down(C - 1, NX - 2, False)
            down(C - 1, NX - 1, False)
            pe.wait_ge(y_ps, NX * C)
            pe.sem_inc(out_ps, 1)
            to_tokens(C - 1, E * C)


_INS = ['x', 'ctx_768', 'L0_xattn_Wq', 'L0_xattn_Wk', 'L0_xattn_Wv', 'L0_xattn_Wo', 'L0_ffn_gate_w', 'L0_ffn_gate_b',
        'L0_ffn_sw1', 'L0_ffn_sb1', 'L0_ffn_sw2', 'L0_ffn_sb2', 'L0_ffn_rw1', 'L0_ffn_rb1', 'L0_ffn_rw2', 'L0_ffn_rb2']
_OUTS = [((8, 256, 128), 'float32')]


def kernel(**inputs):
    import numpy as _np
    import concourse.bacc as _bacc
    from concourse import mybir as _mybir
    from concourse.bass_utils import run_bass_kernel_spmd as _run

    nc = _bacc.Bacc("TRN2", target_bir_lowering=False, num_devices=1)
    arrays, args = {}, []
    for name in _INS:
        a = _np.ascontiguousarray(inputs[name])
        arrays[f"in_{name}_dram"] = a
        args.append(nc.dram_tensor(f"in_{name}_dram", a.shape, _mybir.dt.from_np(a.dtype), kind="ExternalInput").ap())
    for i, (shape, dtype) in enumerate(_OUTS):
        dt = _mybir.dt.from_np(_np.dtype(dtype))
        args.append(nc.dram_tensor(f"out_{i}_dram", shape, dt, kind="ExternalOutput").ap())
    xattn_moe_kernel(nc, *args)
    r = _run(nc, [arrays], core_ids=[0])
    got = tuple(r.results[0][f"out_{i}_dram"] for i in range(len(_OUTS)))
    return got[0]
```

```python
from contextlib import ExitStack

import concourse.bass as bass
from concourse import mybir

F32 = mybir.dt.float32
F32R = mybir.dt.float32r
ALU = mybir.AluOpType
ACT = mybir.ActivationFunctionType
X = mybir.AxisListType.X

P = 128
EPS = 1e-5


def xattn_moe_kernel(nc, x, ctx, wq, wk, wv, wo, gate_w, gate_b, sw1, sb1, sw2, sb2, rw1, rb1, rw2, rb2, out):
    B, S, D = x.shape
    DC = ctx.shape[2]
    E = rw1.shape[0]
    NX = E + 1
    FF = rw2.shape[1]
    IB = S // P
    CB = 2
    TC = CB * IB
    N = TC * P
    C = B // CB
    assert D == P and FF == P and N == 512 and NX % 3 == 0

    with ExitStack() as stack:
        def sb(name, shape, dt=F32):
            return stack.enter_context(nc.sbuf_tensor(name, shape, dt))

        def sem(name):
            return stack.enter_context(nc.semaphore(name))

        bank = [stack.enter_context(nc.psum_tensor(f"bank{i}", [P, 512], F32)) for i in range(8)]

        x_sb = sb("x_sb", [P, B * IB, D])
        ctx_sb = sb("ctx_sb", [P, B * IB, DC])
        wq_sb, wk_sb, wv_sb, wo_sb = sb("wq_sb", [P, D]), sb("wk_sb", [P, DC]), sb("wv_sb", [P, DC]), sb("wo_sb", [P, D])
        w1_sb = sb("w1_sb", [P, NX, 2 * FF])
        w2_sb = sb("w2_sb", [P, NX, D])
        b1_rows = sb("b1_rows", [NX, 2 * FF])
        b2_rows = sb("b2_rows", [P, D])
        sb2_col = sb("sb2_col", [P, 1])
        gate_w_sb = sb("gate_w_sb", [P, P])
        gate_b_col = sb("gate_b_col", [P, 1])

        ident = sb("ident", [P, P])
        mean_of_partitions = sb("mean_of_partitions", [P, P])
        minus_half = sb("minus_half", [P, 8])
        descending = sb("descending", [P, E])
        pick_f = sb("pick_f", [P, E, P])
        pick = sb("pick", [P, E, P], F32R)

        wo_t = sb("wo_t", [P, D])
        qk_w = sb("qk_w", [P, DC])
        vo_w = sb("vo_w", [DC, D])
        b1_cols = sb("b1_cols", [P, 2, NX])
        w1_head, w1_rest = sb("w1_head", [P, NX, 2 * FF], F32R), sb("w1_rest", [P, NX, 2 * FF], F32R)
        w2_head, w2_rest = sb("w2_head", [P, NX, D], F32R), sb("w2_rest", [P, NX, D], F32R)
        b2_head, b2_rest = sb("b2_head", [P, D], F32R), sb("b2_rest", [P, D], F32R)
        gate_head, gate_rest = sb("gate_head", [P, P], F32R), sb("gate_rest", [P, P], F32R)

        ln_stats = sb("ln_stats", [P, 2, TC, 6])
        ln_mv = sb("ln_mv", [P, 2, TC, 2])
        ln_veps = sb("ln_veps", [P, 2, TC])
        ln_rstd = sb("ln_rstd", [P, 2, TC])
        xn = sb("xn", [P, 2, TC, D])
        xn_t = sb("xn_t", [P, N])
        ctx_t = sb("ctx_t", [DC, N])
        t_sb = sb("t_sb", [DC, N])
        v_sb = sb("v_sb", [P, C, TC, D])
        sim_sq = sb("sim_sq", [P, CB])
        row_max = sb("row_max", [P, CB, IB])
        sim_stats = sb("sim_stats", [P, CB, 6])
        sim_mv = sb("sim_mv", [P, CB, 2])
        sim_avg = sb("sim_avg", [P, CB, 2])
        sim_veps = sb("sim_veps", [P, CB])
        sim_r = sb("sim_r", [P, CB])
        neg_max = sb("neg_max", [P, CB, IB])
        prob = sb("prob", [P, CB, IB, S])
        row_sum = sb("row_sum", [P, CB, IB])
        row_inv = sb("row_inv", [P, CB, IB])
        prob_t = sb("prob_t", [P, CB, IB, S])
        x1 = sb("x1", [P, B * IB, D])

        logits_t = sb("logits_t", [E, N])
        logits = sb("logits", [P, TC, E])
        g_sum, g_inv = sb("g_sum", [P, TC]), sb("g_inv", [P, TC])
        g_z, g_exp, g_p = sb("g_z", [P, TC, E]), sb("g_exp", [P, TC, E]), sb("g_p", [P, TC, E])
        g_best = [sb(f"g_best{k}", [P, TC]) for k in range(2)]
        g_first = [sb(f"g_first{k}", [P, TC]) for k in range(2)]
        g_eq = [sb(f"g_eq{k}", [P, TC, E]) for k in range(2)]
        g_rank = [sb(f"g_rank{k}", [P, TC, E]) for k in range(2)]
        g_hot = [sb(f"g_hot{k}", [P, TC, E]) for k in range(2)]
        g_left, g_mask, g_cw = sb("g_left", [P, TC, E]), sb("g_mask", [P, TC, E]), sb("g_cw", [P, TC, E])
        cw_parts = sb("cw_parts", [P, TC, 2, E])

        x2_head = sb("x2_head", [P, C, N], F32R)
        x2_rest = sb("x2_rest", [P, C, N], F32R)
        cw_t = sb("cw_t", [P, C, N], F32R)
        silu = sb("silu", [P, 3, N])
        act = sb("act", [P, 3, N])
        act_head = sb("act_head", [P, 3, N], F32R)
        act_rest = sb("act_rest", [P, 3, N], F32R)
        out_t = sb("out_t", [P, N])

        x_in = [sem(f"x_in{c}") for c in range(C)]
        ctx_in = [sem(f"ctx_in{c}") for c in range(C)]
        attn_w_in, ffn_w_in, small_in, stored = sem("attn_w_in"), sem("ffn_w_in"), sem("small_in"), sem("stored")
        ident_ready, consts_ready, pool_order = sem("ident_ready"), sem("consts_ready"), sem("pool_order")
        w_heads, w_rests = sem("w_heads"), sem("w_rests")
        setup_ps, setup_sb = sem("setup_ps"), sem("setup_sb")
        dve_order = sem("dve_order")
        ln_var, ln_r, xn_ready = [sem("ln1_var"), sem("ln2_var")], [sem("ln1_r"), sem("ln2_r")], [sem("xn1_ready"), sem("xn2_ready")]
        xnt_ps, xnt_sb, ctxt_ps, ctxt_sb = sem("xnt_ps"), sem("xnt_sb"), sem("ctxt_ps"), sem("ctxt_sb")
        t_ps, t_ready, v_ps, v_ready = sem("t_ps"), sem("t_ready"), sem("v_ps"), sem("v_ready")
        sim_ps, simstat_sb, simavg_ps, simavg_sb = sem("sim_ps"), sem("simstat_sb"), sem("simavg_ps"), sem("simavg_sb")
        simvar_sb, simr_sb, negmax_sb = sem("simvar_sb"), sem("simr_sb"), sem("negmax_sb")
        prob_sb, probt_ps, probt_sb, attn_ps, x1_ready = sem("prob_sb"), sem("probt_ps"), sem("probt_sb"), sem("attn_ps"), sem("x1_ready")
        x2t_ps, x2_head_sb, x2_rest_sb = sem("x2t_ps"), sem("x2_head_sb"), sem("x2_rest_sb")
        lgt_ps, lgt_sb, lg_ps, lg_sb = sem("lgt_ps"), sem("lgt_sb"), sem("lg_ps"), sem("lg_sb")
        mask_sb = sem("mask_sb")
        gz_sb, gexp_sb, cw_sb, cwt_ps, cwt_sb = sem("gz_sb"), sem("gexp_sb"), sem("cw_sb"), sem("cwt_ps"), sem("cwt_sb")
        a_ps, b_ps, cw_ps, silu_sb, scaled_sb = sem("a_ps"), sem("b_ps"), sem("cw_ps"), sem("silu_sb"), sem("scaled_sb")
        act_sb, head_sb, rest_sb, y_ps = sem("act_sb"), sem("head_sb"), sem("rest_sb"), sem("y_ps")
        out_ps, outt_sb, tok_ps, final_sb = sem("out_ps"), sem("outt_sb"), sem("tok_ps"), sem("final_sb")

        x_dram = x.rearrange("b (p i) d -> p b i d", i=IB)
        ctx_dram = ctx.rearrange("b (p i) d -> p b i d", i=IB)
        out_dram = out.rearrange("(c b) (p i) d -> c p b (i d)", i=IB, b=CB)

        def tiles(c):
            return slice(TC * c, TC * (c + 1))

        def per_token(v, shape):
            return v.unsqueeze(2).broadcast_to(shape)

        HID, CW_B, OUT_B, PROB, LATE = bank[0:3], bank[3], bank[4], bank[5:7], bank[7]

        def early(c):
            return bank[3:5] if c == 1 else PROB

        GROUPS = [(0, 1), (1, 3), (3, 6), (6, NX)]
        ORDER_OF_SPLITS = 2

        def splits_for(e):
            return ORDER_OF_SPLITS + 2 * (1 + next(g for g, (lo, hi) in enumerate(GROUPS) if lo <= e < hi))

        def split_list():
            yield gate_head[:, :], gate_rest[:, :], gate_w_sb[:, :]
            yield b2_head[:, :], b2_rest[:, :], b2_rows[:, :]
            for lo, hi in GROUPS:
                yield w1_head[:, lo:hi, :], w1_rest[:, lo:hi, :], w1_sb[:, lo:hi, :]
                yield w2_head[:, lo:hi, :], w2_rest[:, lo:hi, :], w2_sb[:, lo:hi, :]

        PE_AT = {"transpose_inputs": (-6, 4), "project": (-5, 4), "scores": (-4, 4), "scores_average": (-1, 3),
                 "transpose_prob": (1, 4), "attend": (2, 4), "transpose_x2": (5, 3), "router": (6, 3),
                 "transpose_logits": (7, 3), "transpose_cw": (10, 3)}
        ACT_AT = {"input_copies": (-5, 0), "projection_copies": (-4, 0), "exponentials": (0, 2), "prob_copies": (2, 0),
                  "x2_heads": (5, 2), "logits_bias": (6, 2), "logits_copy": (7, 2), "router_exp": (9, 2), "cw_copy": (10, 2)}
        DVE_AT = {"first_statistics": (-9, 2), "first_normalise": (-8, 2), "statistics_0": (-3, 2), "statistics_1": (-2, 2),
                  "variance": (-1, 0), "scale": (-1, 2), "residual": (3, 2), "second_normalise": (4, 2), "x2_rests": (5, 2),
                  "router_logits": (7, 2), "router_select": (8, 2), "router_weights": (9, 2)}
        POOL_AT = {"first_rstd": (-8, 0), "scores_rstd": (-1, 0), "second_rstd": (4, 0)}

        def due(table, n, place):
            return [(piece, c) for piece, (slot, where) in table.items() for c in range(C)
                    if where == place and (c - 1) * NX + slot == n]

        block = stack.enter_context(nc.Block())

        @block.sync
        def _(sp):
            def load_x(c):
                sp.dma_start(x_sb[:, tiles(c), :].rearrange("p (b i) d -> p b i d", i=IB),
                             x_dram[:, CB * c:CB * (c + 1)]).then_inc(x_in[c], 16)

            def load_ctx(c):
                sp.dma_start(ctx_sb[:, tiles(c), :].rearrange("p (b i) d -> p b i d", i=IB),
                             ctx_dram[:, CB * c:CB * (c + 1)]).then_inc(ctx_in[c], 16)

            load_x(0)
            for dst, src in ((wq_sb, wq), (wk_sb, wk), (wo_sb, wo), (wv_sb, wv)):
                sp.dma_start(dst[:, :], src).then_inc(attn_w_in, 16)
            load_ctx(0)
            load_x(1)
            load_ctx(1)
            sp.dma_start(b1_rows[0:1, :], sb1).then_inc(small_in, 16)
            sp.dma_start(b1_rows[1:NX, :], rb1).then_inc(small_in, 16)
            sp.dma_start(sb2_col[:, :], sb2.rearrange("a d -> d a")).then_inc(small_in, 16)
            sp.dma_start(gate_b_col[0:E, :], gate_b.rearrange("(e a) -> e a", a=1)).then_inc(small_in, 16)
            sp.wait_ge(consts_ready, 1)
            sp.dma_start(b2_rows[0:E, :], rb2).then_inc(small_in, 16)
            sp.dma_start(b2_rows[E:2 * E, :], rb2).then_inc(small_in, 16)
            sp.dma_start(gate_w_sb[:, 0:E], gate_w).then_inc(small_in, 16)
            sp.dma_start(w1_sb[:, 0, :], sw1[0]).then_inc(ffn_w_in, 16)
            sp.dma_start(w2_sb[:, 0, :], sw2[0]).then_inc(ffn_w_in, 16)
            sp.dma_start(w1_sb[:, 1:NX, :], rw1.rearrange("e d f -> d e f")).then_inc(ffn_w_in, 16)
            sp.dma_start(w2_sb[:, 1:NX, :], rw2.rearrange("e f d -> f e d")).then_inc(ffn_w_in, 16)
            for c in range(2, C):
                load_x(c)
                load_ctx(c)
            for c in range(C):
                sp.wait_ge(final_sb, c + 1)
                sp.dma_start(out_dram[c], x1[:, tiles(c), :].rearrange("p (b i) d -> p b (i d)", i=IB)).then_inc(stored, 16)
            sp.wait_ge(stored, 16 * C)

        @block.gpsimd
        def _(pool):
            order = [0]

            def wait_own(ins):
                order[0] += 1
                ins.then_inc(pool_order, 1)
                pool.wait_ge(pool_order, order[0])

            def rstd(which, c):
                pool.wait_ge(ln_var[which], c + 1)
                if c >= 1:
                    pool.wait_ge(xn_ready[which], c)
                pool.tensor_tensor(ln_rstd[:, which, :], ln_veps[:, which, :], minus_half[:, 0:TC], ALU.pow).then_inc(ln_r[which], 1)

            def scores_rstd(c):
                pool.wait_ge(simvar_sb, c + 1)
                if c >= 1:
                    pool.wait_ge(prob_sb, CB * c)
                pool.tensor_tensor(sim_r[:, :], sim_veps[:, :], minus_half[:, 0:CB], ALU.pow).then_inc(simr_sb, 1)

            def split_rests(lo, hi):
                for k, (head, rest, whole) in enumerate(split_list()):
                    if lo <= k < hi:
                        pool.wait_ge(w_heads, k + 1)
                        pool.tensor_tensor(rest, whole, head.bitcast(F32), ALU.subtract).then_inc(w_rests, 1)

            def expert_rest(c, e):
                n, k = NX * c + e, e % 3
                pool.wait_ge(head_sb, n + 1)
                if n >= 3:
                    pool.wait_ge(y_ps, n - 2)
                pool.tensor_tensor(act_rest[:, k, :], act[:, k, :], act_head[:, k, :].bitcast(F32), ALU.subtract).then_inc(rest_sb, 1)

            wait_own(pool.memset(minus_half[:, :], -0.5))
            wait_own(pool.memset(ident[:, :], 0.0))
            pool.affine_select(out=ident[:, :], in_=ident[:, :], compare_op=ALU.not_equal, fill=1.0, base=0,
                               pattern=[[-1, P]], channel_multiplier=1).then_inc(ident_ready, 1)
            wait_own(pool.memset(gate_w_sb[:, :], 0.0))
            wait_own(pool.memset(b2_rows[:, :], 0.0))
            pool.memset(mean_of_partitions[:, :], 1.0 / P).then_inc(consts_ready, 1)
            rstd(0, 0)
            for k in range(E):
                pool.memset(descending[:, k:k + 1], float(E - k)).then_inc(consts_ready, 1)
            rstd(0, 1)
            pool.memset(cw_t[:, :, :].bitcast(F32), 0.0).then_inc(consts_ready, 1)
            wait_own(pool.memset(pick_f[:, :, :], 0.0))
            for base in (0, -E):
                wait_own(pool.affine_select(out=pick_f[:, :, :], in_=pick_f[:, :, :], compare_op=ALU.not_equal, fill=1.0,
                                            base=base, pattern=[[-1, E], [0, P]], channel_multiplier=1))
            scores_rstd(0)
            split_rests(0, 2)
            rstd(1, 0)
            split_rests(2, 6)
            scores_rstd(1)
            pool.tensor_copy(pick[:, :, :], pick_f[:, :, :]).then_inc(consts_ready, 1)
            pieces = {"first_rstd": lambda c: rstd(0, c), "second_rstd": lambda c: rstd(1, c), "scores_rstd": scores_rstd}
            for n in range(NX * C):
                for piece, c in due(POOL_AT, n, 0):
                    pieces[piece](c)
                if n in (0, 2):
                    split_rests(6 + n, 8 + n)
                expert_rest(n // NX, n % NX)
                for piece, c in due(POOL_AT, n, 1):
                    pieces[piece](c)

        @block.scalar
        def _(scalar):
            copy = scalar.copy

            def xn_copy(c):
                scalar.wait_ge(xnt_ps, c + 1)
                if c >= 1:
                    scalar.wait_ge(t_ps, c)
                copy(xn_t[:, :], early(c)[0][:, :]).then_inc(xnt_sb, 1)

            def ctx_copy(c):
                scalar.wait_ge(ctxt_ps, c + 1)
                if c >= 1:
                    scalar.wait_ge(sim_ps, CB * c)
                copy(ctx_t[:, :], early(c)[1][0:DC, :]).then_inc(ctxt_sb, 1)

            def t_copy(c):
                scalar.wait_ge(t_ps, c + 1)
                if c >= 1:
                    scalar.wait_ge(sim_ps, CB * c)
                copy(t_sb[:, :], early(c)[0][0:DC, :]).then_inc(t_ready, 1)

            def v_copy(c):
                scalar.wait_ge(v_ps, c + 1)
                copy(v_sb[:, c].rearrange("p t d -> p (t d)"), early(c)[1][:, :]).then_inc(v_ready, 1)

            def exponentials(c):
                scalar.wait_ge(negmax_sb, c + 1)
                if c >= 1:
                    scalar.wait_ge(probt_ps, CB * c)
                    scalar.wait_ge(x1_ready, c)
                for j in range(CB):
                    for i in range(IB):
                        last = scalar.activation(prob[:, j, i, :], early(c)[j][:, i * S:(i + 1) * S], ACT.Exp,
                                                 bias=neg_max[:, j, i:i + 1], scale=sim_r[:, j:j + 1],
                                                 accum_out=row_sum[:, j, i:i + 1])
                    last.then_inc(prob_sb, 1)

            def prob_copy(m):
                j = m % CB
                scalar.wait_ge(probt_ps, m + 1)
                if m >= CB:
                    scalar.wait_ge(attn_ps, m // CB)
                copy(prob_t[:, j].rearrange("p k q -> p (k q)"), PROB[j][:, :]).then_inc(probt_sb, 1)

            def x2_heads(c):
                scalar.wait_ge(x2t_ps, c + 1)
                copy(x2_head[:, c, :], LATE[:, :]).then_inc(x2_head_sb, 1)

            def logits_bias(c):
                scalar.wait_ge(lgt_ps, c + 1)
                if c >= 1:
                    scalar.wait_ge(lg_ps, c)
                scalar.activation(logits_t[:, :], LATE[0:E, :], ACT.Identity, bias=gate_b_col[0:E, :]).then_inc(lgt_sb, 1)

            def logits_copy(c):
                scalar.wait_ge(lg_ps, c + 1)
                if c >= 1:
                    scalar.wait_ge(gz_sb, c)
                copy(logits[:, :, :].rearrange("p t e -> p (t e)"), LATE[:, 0:TC * E]).then_inc(lg_sb, 1)

            def router_exp(c):
                scalar.wait_ge(gz_sb, c + 1)
                if c >= 1:
                    scalar.wait_ge(cw_sb, c)
                scalar.activation(g_exp[:, :, :], g_z[:, :, :], ACT.Exp).then_inc(gexp_sb, 1)

            def cw_copy(c):
                scalar.wait_ge(cwt_ps, c + 1)
                if c == 0:
                    scalar.wait_ge(consts_ready, 2 + E)
                copy(cw_t[0:2 * E, c, :], LATE[0:2 * E, :]).then_inc(cwt_sb, 1)

            def split_heads(lo, hi):
                for k, (head, _, whole) in enumerate(split_list()):
                    if lo <= k < hi:
                        copy(head, whole).then_inc(w_heads, 1)

            def expert_silu(c, e):
                n, k = NX * c + e, e % 3
                scalar.wait_ge(a_ps, n + 1)
                if n >= 3:
                    scalar.wait_ge(act_sb, n - 2)
                scalar.activation(silu[:, k, :], HID[(2 * n) % 3][:, :], ACT.Silu, bias=b1_cols[:, 0, e:e + 1]).then_inc(silu_sb, 1)

            def expert_head(n):
                k = n % 3
                scalar.wait_ge(act_sb, n + 1)
                if n >= 3:
                    scalar.wait_ge(y_ps, n - 2)
                copy(act_head[:, k, :], act[:, k, :]).then_inc(head_sb, 1)

            def out_bias(c):
                scalar.wait_ge(y_ps, NX * (c + 1))
                if c >= 1:
                    scalar.wait_ge(tok_ps, c)
                scalar.activation(out_t[:, :], OUT_B[:, :], ACT.Identity, bias=sb2_col[:, :]).then_inc(outt_sb, 1)

            scalar.wait_ge(setup_ps, 1)
            copy(wo_t[:, :], bank[0][:, 0:D]).then_inc(setup_sb, 1)
            scalar.wait_ge(setup_ps, 2)
            copy(qk_w[:, :], bank[1][:, 0:DC]).then_inc(setup_sb, 1)
            scalar.wait_ge(setup_ps, 3)
            copy(vo_w[:, :], bank[2][0:DC, 0:D]).then_inc(setup_sb, 1)
            ctx_copy(0)
            xn_copy(0)
            v_copy(0)
            t_copy(0)
            scalar.wait_ge(small_in, 16 * 7)
            scalar.wait_ge(setup_ps, 4)
            copy(b1_cols[:, :, :].rearrange("p h e -> p (h e)"), bank[0][:, 0:2 * NX]).then_inc(setup_sb, 1)
            xn_copy(1)
            ctx_copy(1)
            split_heads(0, 2)
            exponentials(0)
            prob_copy(0)
            prob_copy(1)
            t_copy(1)
            v_copy(1)
            scalar.wait_ge(ffn_w_in, 64)
            split_heads(2, 6)
            x2_heads(0)
            split_heads(6, 10)
            logits_bias(0)
            logits_copy(0)

            def input_copies(c):
                xn_copy(c)
                ctx_copy(c)

            def projection_copies(c):
                t_copy(c)
                v_copy(c)

            def prob_copies(c):
                for j in range(CB):
                    prob_copy(CB * c + j)

            pieces = {"input_copies": input_copies, "projection_copies": projection_copies, "exponentials": exponentials,
                      "prob_copies": prob_copies, "x2_heads": x2_heads, "logits_bias": logits_bias,
                      "logits_copy": logits_copy, "router_exp": router_exp, "cw_copy": cw_copy}
            for n in range(NX * C):
                c, e = n // NX, n % NX
                if e == 2 and c >= 1:
                    out_bias(c - 1)
                for piece, k in due(ACT_AT, n, 0):
                    pieces[piece](k)
                expert_silu(c, e)
                for piece, k in due(ACT_AT, n, 1):
                    pieces[piece](k)
                if n >= 1:
                    expert_head(n - 1)
                for piece, k in due(ACT_AT, n, 2):
                    pieces[piece](k)
            expert_head(NX * C - 1)
            out_bias(C - 1)

        @block.vector
        def _(dve):
            order = [0]

            def own(ins):
                order[0] += 1
                return ins.then_inc(dve_order, 1)

            def wait_own():
                dve.wait_ge(dve_order, order[0])

            def ln_statistics(which, c, src):
                for i in range(TC):
                    own(dve.bn_stats(ln_stats[:, which, i, :], src[:, TC * c + i, :]))
                wait_own()
                for i in range(TC):
                    own(dve.bn_aggr(ln_mv[:, which, i, :], ln_stats[:, which, i, :]))
                wait_own()
                if c >= 1:
                    dve.wait_ge(ln_r[which], c)
                dve.tensor_scalar(ln_veps[:, which, :], ln_mv[:, which, :, 1], EPS, None, ALU.add).then_inc(ln_var[which], 1)

            def ln_normalise(which, c, src, transposed):
                dve.wait_ge(ln_r[which], c + 1)
                if c >= 1:
                    dve.wait_ge(transposed, c)
                for i in range(TC):
                    last = dve.tensor_scalar(xn[:, which, i, :], src[:, TC * c + i, :], ln_mv[:, which, i, 0:1],
                                             ln_rstd[:, which, i:i + 1], ALU.subtract, ALU.mult)
                last.then_inc(xn_ready[which], 1)

            def scores_statistics(m):
                j = m % CB
                scores = early(m // CB)[j]
                dve.wait_ge(sim_ps, m + 1)
                own(dve.tensor_reduce(row_max[:, j, :], scores[:, :].rearrange("p (i k) -> p i k", i=IB), X, ALU.max))
                own(dve.bn_stats(sim_stats[:, j, :], scores[:, :]))
                wait_own()
                own(dve.bn_aggr(sim_mv[:, j, :], sim_stats[:, j, :]))

            def scores_squares(c):
                wait_own()
                own(dve.tensor_tensor(sim_sq[:, :], sim_mv[:, :, 0], sim_mv[:, :, 0], ALU.mult))
                wait_own()
                dve.tensor_tensor(sim_mv[:, :, 1], sim_sq[:, :], sim_mv[:, :, 1], ALU.add).then_inc(simstat_sb, 1)

            def scores_variance(c):
                dve.wait_ge(simavg_ps, c + 1)
                dve.tensor_copy(sim_avg[:, :, :].rearrange("p j k -> p (j k)"), LATE[:, 0:2 * CB]).then_inc(simavg_sb, 1)
                dve.wait_ge(simavg_sb, c + 1)
                own(dve.tensor_tensor(sim_sq[:, :], sim_avg[:, :, 0], sim_avg[:, :, 0], ALU.mult))
                wait_own()
                dve.scalar_tensor_tensor(sim_veps[:, :], sim_avg[:, :, 1], EPS, sim_sq[:, :],
                                         ALU.add, ALU.subtract).then_inc(simvar_sb, 1)

            def scores_scale(c):
                dve.wait_ge(simr_sb, c + 1)
                if c >= 1:
                    dve.wait_ge(prob_sb, CB * c)
                for j in range(CB):
                    last = dve.tensor_scalar(neg_max[:, j, :], row_max[:, j, :], sim_r[:, j:j + 1], -1.0, ALU.mult, ALU.mult)
                last.then_inc(negmax_sb, 1)

            def residual(c):
                dve.wait_ge(prob_sb, CB * (c + 1))
                own(dve.reciprocal(row_inv[:, :, :], row_sum[:, :, :]))
                wait_own()
                dve.wait_ge(attn_ps, c + 1)
                for i in range(TC):
                    last = dve.scalar_tensor_tensor(x1[:, TC * c + i, :], LATE[:, i * D:(i + 1) * D],
                                                    row_inv[:, i // IB, i % IB:i % IB + 1], x_sb[:, TC * c + i, :],
                                                    ALU.mult, ALU.add)
                last.then_inc(x1_ready, 1)

            def second_statistics(c):
                dve.wait_ge(x1_ready, c + 1)
                ln_statistics(1, c, x1)

            def x2_rests(c):
                dve.wait_ge(x2_head_sb, c + 1)
                dve.tensor_tensor(x2_rest[:, c, :], LATE[:, :], x2_head[:, c, :].bitcast(F32), ALU.subtract).then_inc(x2_rest_sb, 1)

            full = [P, TC, E]

            def router_logits(c):
                dve.wait_ge(lg_sb, c + 1)
                own(dve.tensor_reduce(g_best[0][:, :], logits[:, :, :], X, ALU.max))
                wait_own()
                if c >= 1:
                    dve.wait_ge(gexp_sb, c)
                dve.tensor_tensor(g_z[:, :, :], logits[:, :, :], per_token(g_best[0][:, :], full), ALU.subtract).then_inc(gz_sb, 1)

            def router_select(c):
                for k, left in enumerate((logits, g_left)):
                    if k == 1:
                        own(dve.scalar_tensor_tensor(g_left[:, :, :], g_hot[0][:, :, :], -3.0e38, logits[:, :, :], ALU.mult, ALU.add))
                        wait_own()
                        own(dve.tensor_reduce(g_best[1][:, :], g_left[:, :, :], X, ALU.max))
                        wait_own()
                    own(dve.tensor_tensor(g_eq[k][:, :, :], left[:, :, :], per_token(g_best[k][:, :], full), ALU.is_ge))
                    wait_own()
                    own(dve.tensor_tensor(g_rank[k][:, :, :], g_eq[k][:, :, :],
                                          descending[:, :].unsqueeze(1).broadcast_to(full), ALU.mult))
                    wait_own()
                    own(dve.tensor_reduce(g_first[k][:, :], g_rank[k][:, :, :], X, ALU.max))
                    wait_own()
                    own(dve.tensor_tensor(g_hot[k][:, :, :], g_rank[k][:, :, :], per_token(g_first[k][:, :], full), ALU.is_equal))
                    wait_own()
                dve.tensor_tensor(g_mask[:, :, :], g_hot[0][:, :, :], g_hot[1][:, :, :], ALU.add).then_inc(mask_sb, 1)

            def router_weights(c):
                dve.wait_ge(gexp_sb, c + 1)
                dve.wait_ge(mask_sb, c + 1)
                own(dve.tensor_reduce(g_sum[:, :], g_exp[:, :, :], X, ALU.add))
                own(dve.tensor_tensor(g_p[:, :, :], g_exp[:, :, :], g_mask[:, :, :], ALU.mult))
                wait_own()
                own(dve.reciprocal(g_inv[:, :], g_sum[:, :]))
                wait_own()
                if c >= 1:
                    dve.wait_ge(cwt_ps, c)
                own(dve.tensor_tensor(cw_parts[:, :, 0, :].bitcast(F32R), g_p[:, :, :], per_token(g_inv[:, :], full), ALU.mult))
                own(dve.tensor_tensor(g_cw[:, :, :], g_p[:, :, :], per_token(g_inv[:, :], full), ALU.mult))
                wait_own()
                dve.tensor_tensor(cw_parts[:, :, 1, :], g_cw[:, :, :], cw_parts[:, :, 0, :], ALU.subtract).then_inc(cw_sb, 1)

            def expert_gate(c, e, between):
                n, k = NX * c + e, e % 3
                dve.wait_ge(silu_sb, n + 1)
                if e >= 1:
                    dve.wait_ge(cw_ps, E * c + e)
                    dve.tensor_tensor(silu[:, k, :], silu[:, k, :], CW_B[:, :], ALU.mult).then_inc(scaled_sb, 1)
                between()
                if e >= 1:
                    dve.wait_ge(scaled_sb, E * c + e)
                dve.wait_ge(b_ps, n + 1)
                if n >= 3:
                    dve.wait_ge(rest_sb, n - 2)
                dve.scalar_tensor_tensor(act[:, k, :], HID[(2 * n + 1) % 3][:, :], b1_cols[:, 1, e:e + 1], silu[:, k, :],
                                         ALU.add, ALU.mult).then_inc(act_sb, 1)

            def final(c):
                dve.wait_ge(tok_ps, c + 1)
                rows = x1[:, tiles(c), :].rearrange("p t d -> p (t d)")
                dve.tensor_tensor(rows, CW_B[:, :], rows, ALU.add).then_inc(final_sb, 1)

            for c in range(2):
                dve.wait_ge(x_in[c], 16)
                ln_statistics(0, c, x_sb)
                ln_normalise(0, c, x_sb, xnt_ps)
            scores_statistics(0)
            scores_statistics(1)
            scores_squares(0)
            scores_variance(0)
            scores_scale(0)
            dve.wait_ge(consts_ready, 1 + E)
            residual(0)
            second_statistics(0)
            ln_normalise(1, 0, x1, x2t_ps)
            scores_statistics(CB)
            x2_rests(0)
            scores_statistics(CB + 1)
            scores_squares(1)
            scores_variance(1)
            scores_scale(1)
            router_logits(0)
            router_select(0)
            dve.wait_ge(setup_sb, 4)

            def first_statistics(c):
                dve.wait_ge(x_in[c], 16)
                ln_statistics(0, c, x_sb)

            def attention_output(c):
                residual(c)
                second_statistics(c)

            def statistics_1(c):
                scores_statistics(CB * c + 1)
                scores_squares(c)

            pieces = {"first_statistics": first_statistics, "first_normalise": lambda c: ln_normalise(0, c, x_sb, xnt_ps),
                      "statistics_0": lambda c: scores_statistics(CB * c), "statistics_1": statistics_1,
                      "variance": scores_variance, "scale": scores_scale, "residual": attention_output,
                      "second_normalise": lambda c: ln_normalise(1, c, x1, x2t_ps), "x2_rests": x2_rests,
                      "router_logits": router_logits, "router_select": router_select, "router_weights": router_weights}

            def run(n, place):
                for piece, c in due(DVE_AT, n, place):
                    pieces[piece](c)

            for n in range(NX * C):
                c, e = n // NX, n % NX
                if e == 3 and c >= 1:
                    final(c - 1)
                run(n, 0)
                expert_gate(c, e, lambda: run(n, 1))
                run(n, 2)
            final(C - 1)

        @block.tensor
        def _(pe):
            def mm(dst, lhs, rhs, start=True, stop=True):
                return pe.matmul(dst, lhs, rhs, start=start, stop=stop, skip_group_check=True)

            def transpose_x(c):
                pe.wait_ge(xn_ready[0], c + 1)
                if c >= 2:
                    pe.wait_ge(probt_sb, CB * c - 1)
                for i in range(TC):
                    last = pe.transpose(early(c)[0][:, i * P:(i + 1) * P], xn[:, 0, i, :], ident[:, :])
                last.then_inc(xnt_ps, 1)

            def transpose_ctx(c):
                pe.wait_ge(ctx_in[c], 16)
                if c >= 2:
                    pe.wait_ge(probt_sb, CB * c)
                for i in range(TC):
                    last = pe.transpose(early(c)[1][0:DC, i * P:(i + 1) * P], ctx_sb[:, TC * c + i, :], ident[:, :])
                last.then_inc(ctxt_ps, 1)

            def project_q(c):
                pe.wait_ge(xnt_sb, c + 1)
                mm(early(c)[0][0:DC, :], qk_w[:, :], xn_t[:, :]).then_inc(t_ps, 1)

            def project_v(c):
                pe.wait_ge(ctxt_sb, c + 1)
                for i in range(TC):
                    last = mm(early(c)[1][:, i * D:(i + 1) * D], ctx_t[:, i * P:(i + 1) * P], vo_w[:, :])
                last.then_inc(v_ps, 1)

            def scores(c):
                pe.wait_ge(t_ready, c + 1)
                pe.wait_ge(ctxt_sb, c + 1)
                pe.wait_ge(v_ready, c + 1)
                for j in range(CB):
                    for i in range(IB):
                        q = (IB * j + i) * P
                        last = mm(early(c)[j][:, i * S:(i + 1) * S], t_sb[:, q:q + P], ctx_t[:, j * S:(j + 1) * S])
                    last.then_inc(sim_ps, 1)

            def scores_average(c):
                pe.wait_ge(simstat_sb, c + 1)
                if c == 0:
                    pe.wait_ge(consts_ready, 1)
                else:
                    pe.wait_ge(lg_sb, c)
                mm(LATE[:, 0:2 * CB], mean_of_partitions[:, :], sim_mv[:, :, :].rearrange("p j k -> p (j k)")).then_inc(simavg_ps, 1)

            def transpose_prob(c):
                pe.wait_ge(prob_sb, CB * (c + 1))
                for j in range(CB):
                    for k in range(IB):
                        for i in range(IB):
                            last = pe.transpose(PROB[j][:, k * S + i * P:k * S + (i + 1) * P],
                                                prob[:, j, i, k * P:(k + 1) * P], ident[:, :])
                    last.then_inc(probt_ps, 1)

            def attend(c):
                pe.wait_ge(v_ready, c + 1)
                if c >= 1:
                    pe.wait_ge(cwt_sb, c)
                for j in range(CB):
                    pe.wait_ge(probt_sb, CB * c + j + 1)
                    for i in range(IB):
                        for k in range(IB):
                            last = mm(LATE[:, (IB * j + i) * D:(IB * j + i + 1) * D], prob_t[:, j, k, i * P:(i + 1) * P],
                                      v_sb[:, c, IB * j + k, :], start=k == 0, stop=k == IB - 1)
                last.then_inc(attn_ps, 1)

            def transpose_x2(c):
                pe.wait_ge(xn_ready[1], c + 1)
                pe.wait_ge(x1_ready, c + 1)
                for i in range(TC):
                    last = pe.transpose(LATE[:, i * P:(i + 1) * P], xn[:, 1, i, :], ident[:, :])
                last.then_inc(x2t_ps, 1)

            def router(c):
                pe.wait_ge(x2_head_sb, c + 1)
                pe.wait_ge(x2_rest_sb, c + 1)
                if c == 0:
                    pe.wait_ge(w_rests, 1)
                parts = [(g, xs) for g in (gate_head, gate_rest) for xs in (x2_head, x2_rest)]
                for k, (g, xs) in enumerate(parts):
                    last = mm(LATE[:, :], g[:, :], xs[:, c, :], start=k == 0, stop=k == 3)
                last.then_inc(lgt_ps, 1)

            def transpose_logits(c):
                pe.wait_ge(lgt_sb, c + 1)
                for i in range(TC):
                    last = pe.transpose(LATE[:, i * E:(i + 1) * E], logits_t[:, i * P:(i + 1) * P], ident[0:E, 0:E])
                last.then_inc(lg_ps, 1)

            def transpose_cw(c):
                pe.wait_ge(cw_sb, c + 1)
                pe.wait_ge(lg_sb, c + 1)
                if c + 1 < C:
                    pe.wait_ge(simavg_sb, c + 2)
                for i in range(TC):
                    last = pe.transpose(LATE[0:2 * E, i * P:(i + 1) * P], cw_parts[:, i].rearrange("p h e -> p (h e)"), ident[:, :])
                last.then_inc(cwt_ps, 1)

            def hidden(c, e, half):
                n = NX * c + e
                dst = HID[(2 * n + half) % 3]
                cols = slice(half * FF, (half + 1) * FF)
                if half == 0 and n >= 2:
                    pe.wait_ge(act_sb, n - 1)
                if half == 1 and n >= 1:
                    pe.wait_ge(silu_sb, n)
                mm(dst[:, :], w1_head[:, e, cols], x2_head[:, c, :], True, False)
                mm(dst[:, :], w1_head[:, e, cols], x2_rest[:, c, :], False, False)
                mm(dst[:, :], w1_rest[:, e, cols], x2_head[:, c, :], False, True).then_inc((a_ps, b_ps)[half], 1)

            def spread_cw(c, e):
                if E * c + e == 1:
                    pe.wait_ge(prob_sb, 2 * CB)
                else:
                    pe.wait_ge(scaled_sb, E * c + e - 1)
                if e == 1:
                    pe.wait_ge(cwt_sb, c + 1)
                    if c == 0:
                        pe.wait_ge(consts_ready, 3 + E)
                if e == 3 and c >= 1:
                    pe.wait_ge(final_sb, c)
                mm(CW_B[:, :], pick[:, e - 1, :], cw_t[:, c, :]).then_inc(cw_ps, 1)

            def down(n):
                c, e, k = n // NX, n % NX, n % 3
                pe.wait_ge(head_sb, n + 1)
                pe.wait_ge(rest_sb, n + 1)
                if e == 0 and c >= 1:
                    pe.wait_ge(outt_sb, c)
                if e == 1:
                    if c == 0:
                        pe.wait_ge(w_rests, 2)
                    mm(OUT_B[:, :], b2_head[:, :], cw_t[:, c, :], False, False)
                    mm(OUT_B[:, :], b2_rest[:, :], cw_t[:, c, :], False, False)
                mm(OUT_B[:, :], w2_head[:, e, :], act_head[:, k, :], e == 0, False)
                mm(OUT_B[:, :], w2_head[:, e, :], act_rest[:, k, :], False, False)
                mm(OUT_B[:, :], w2_rest[:, e, :], act_head[:, k, :], False, e == NX - 1).then_inc(y_ps, 1)

            def to_tokens(c, cw_used):
                pe.wait_ge(outt_sb, c + 1)
                pe.wait_ge(scaled_sb, cw_used)
                for i in range(TC):
                    last = pe.transpose(CW_B[:, i * P:(i + 1) * P], out_t[:, i * P:(i + 1) * P], ident[:, :])
                last.then_inc(tok_ps, 1)

            pe.wait_ge(ident_ready, 1)
            pe.wait_ge(attn_w_in, 64)
            pe.transpose(bank[0][:, 0:D], wo_sb[:, :], ident[:, :]).then_inc(setup_ps, 1)
            mm(bank[1][:, 0:DC], wq_sb[:, :], wk_sb[:, :]).then_inc(setup_ps, 1)
            pe.wait_ge(setup_sb, 1)
            mm(bank[2][0:DC, 0:D], wv_sb[:, :], wo_t[:, :]).then_inc(setup_ps, 1)
            transpose_ctx(0)
            transpose_x(0)
            pe.wait_ge(setup_sb, 3)
            project_v(0)
            project_q(0)
            scores(0)
            transpose_x(1)
            transpose_ctx(1)
            pe.wait_ge(small_in, 16 * 7)
            for h in range(2):
                last = pe.transpose(bank[0][:, h * NX:(h + 1) * NX], b1_rows[:, h * FF:(h + 1) * FF], ident[0:NX, 0:NX])
            last.then_inc(setup_ps, 1)
            scores_average(0)
            project_q(1)
            project_v(1)
            transpose_prob(0)
            attend(0)
            scores(1)
            transpose_x2(0)
            router(0)
            transpose_logits(0)
            scores_average(1)
            pe.wait_ge(setup_sb, 4)

            def transpose_inputs(c):
                transpose_x(c)
                transpose_ctx(c)

            def project(c):
                project_q(c)
                project_v(c)

            pieces = {"transpose_inputs": transpose_inputs, "project": project, "scores": scores,
                      "scores_average": scores_average, "transpose_prob": transpose_prob, "attend": attend,
                      "transpose_x2": transpose_x2, "router": router, "transpose_logits": transpose_logits,
                      "transpose_cw": transpose_cw}

            def run(n, place):
                for piece, c in due(PE_AT, n, place):
                    pieces[piece](c)

            for n in range(NX * C):
                c, e = n // NX, n % NX
                if c == 0:
                    pe.wait_ge(w_rests, splits_for(e))
                run(n, 0)
                hidden(c, e, 0)
                if e == 3 and c >= 1:
                    to_tokens(c - 1, E * c + e - 1)
                run(n, 1)
                hidden(c, e, 1)
                run(n, 2)
                if e not in (0, 1, 3):
                    spread_cw(c, e)
                run(n, 3)
                if n >= 2:
                    down(n - 2)
                if e in (1, 3):
                    spread_cw(c, e)
                run(n, 4)
            down(NX * C - 2)
            down(NX * C - 1)
            to_tokens(C - 1, E * C)


_INS = ['x', 'ctx_768', 'L0_xattn_Wq', 'L0_xattn_Wk', 'L0_xattn_Wv', 'L0_xattn_Wo', 'L0_ffn_gate_w', 'L0_ffn_gate_b',
        'L0_ffn_sw1', 'L0_ffn_sb1', 'L0_ffn_sw2', 'L0_ffn_sb2', 'L0_ffn_rw1', 'L0_ffn_rb1', 'L0_ffn_rw2', 'L0_ffn_rb2']
_OUTS = [((8, 256, 128), 'float32')]


def kernel(**inputs):
    import numpy as _np
    import concourse.bacc as _bacc
    from concourse import mybir as _mybir
    from concourse.bass_utils import run_bass_kernel_spmd as _run

    nc = _bacc.Bacc("TRN2", target_bir_lowering=False, num_devices=1)
    arrays, args = {}, []
    for name in _INS:
        a = _np.ascontiguousarray(inputs[name])
        arrays[f"in_{name}_dram"] = a
        args.append(nc.dram_tensor(f"in_{name}_dram", a.shape, _mybir.dt.from_np(a.dtype), kind="ExternalInput").ap())
    for i, (shape, dtype) in enumerate(_OUTS):
        dt = _mybir.dt.from_np(_np.dtype(dtype))
        args.append(nc.dram_tensor(f"out_{i}_dram", shape, dt, kind="ExternalOutput").ap())
    xattn_moe_kernel(nc, *args)
    r = _run(nc, [arrays], core_ids=[0])
    got = tuple(r.results[0][f"out_{i}_dram"] for i in range(len(_OUTS)))
    return got[0]
```

```python
from contextlib import ExitStack

import concourse.bass as bass
from concourse import mybir

F32 = mybir.dt.float32
F32R = mybir.dt.float32r
ALU = mybir.AluOpType
ACT = mybir.ActivationFunctionType
X = mybir.AxisListType.X

P = 128
EPS = 1e-5


def xattn_moe_kernel(nc, x, ctx, wq, wk, wv, wo, gate_w, gate_b, sw1, sb1, sw2, sb2, rw1, rb1, rw2, rb2, out):
    B, S, D = x.shape
    DC = ctx.shape[2]
    E = rw1.shape[0]
    NX = E + 1
    FF = rw2.shape[1]
    IB = S // P
    CB = 2
    TC = CB * IB
    N = TC * P
    C = B // CB
    assert D == P and FF == P and N == 512 and NX % 3 == 0

    with ExitStack() as stack:
        def sb(name, shape, dt=F32):
            return stack.enter_context(nc.sbuf_tensor(name, shape, dt))

        def sem(name):
            return stack.enter_context(nc.semaphore(name))

        bank = [stack.enter_context(nc.psum_tensor(f"bank{i}", [P, 512], F32)) for i in range(8)]

        x_sb = sb("x_sb", [P, B * IB, D])
        ctx_sb = sb("ctx_sb", [P, B * IB, DC])
        wq_sb, wk_sb, wv_sb, wo_sb = sb("wq_sb", [P, D]), sb("wk_sb", [P, DC]), sb("wv_sb", [P, DC]), sb("wo_sb", [P, D])
        w1_sb = sb("w1_sb", [P, NX, 2 * FF])
        w2_sb = sb("w2_sb", [P, NX, D])
        b1_rows = sb("b1_rows", [NX, 2 * FF])
        b2_rows = sb("b2_rows", [P, D])
        sb2_col = sb("sb2_col", [P, 1])
        gate_w_sb = sb("gate_w_sb", [P, E])
        gate_b_sb = sb("gate_b_sb", [P, E])

        ident = sb("ident", [P, P])
        mean_of_partitions = sb("mean_of_partitions", [P, P])
        minus_half = sb("minus_half", [P, 8])
        descending = sb("descending", [P, E])
        pick_f = sb("pick_f", [P, E, P])
        pick = sb("pick", [P, E, P], F32R)

        wo_t = sb("wo_t", [P, D])
        qk_w = sb("qk_w", [P, DC])
        vo_w = sb("vo_w", [DC, D])
        b1_cols = sb("b1_cols", [P, 2, NX])
        w1_head, w1_rest = sb("w1_head", [P, NX, 2 * FF], F32R), sb("w1_rest", [P, NX, 2 * FF], F32R)
        w2_head, w2_rest = sb("w2_head", [P, NX, D], F32R), sb("w2_rest", [P, NX, D], F32R)
        b2_head, b2_rest = sb("b2_head", [P, D], F32R), sb("b2_rest", [P, D], F32R)
        gate_parts = sb("gate_parts", [P, 2, E], F32R)

        ln_stats = sb("ln_stats", [P, 2, TC, 6])
        ln_mv = sb("ln_mv", [P, 2, TC, 2])
        ln_veps = sb("ln_veps", [P, 2, TC])
        ln_rstd = sb("ln_rstd", [P, 2, TC])
        xn = sb("xn", [P, 2, TC, D])
        xn_t = sb("xn_t", [P, N])
        ctx_t = sb("ctx_t", [DC, N])
        t_sb = sb("t_sb", [DC, N])
        v_sb = sb("v_sb", [P, C, TC, D])
        sim_sq = sb("sim_sq", [P, CB])
        row_max = sb("row_max", [P, CB, IB])
        sim_stats = sb("sim_stats", [P, CB, 6])
        sim_mv = sb("sim_mv", [P, CB, 2])
        sim_avg = sb("sim_avg", [P, CB, 2])
        sim_veps = sb("sim_veps", [P, CB])
        sim_r = sb("sim_r", [P, CB])
        neg_max = sb("neg_max", [P, CB, IB])
        prob = sb("prob", [P, CB, IB, S])
        row_sum = sb("row_sum", [P, CB, IB])
        row_inv = sb("row_inv", [P, CB, IB])
        prob_t = sb("prob_t", [P, CB, IB, S])
        x1 = sb("x1", [P, B * IB, D])

        logits_part = sb("logits_part", [P, TC, E])
        logits = sb("logits", [P, TC, E])
        g_sum, g_inv = sb("g_sum", [P, TC]), sb("g_inv", [P, TC])
        g_z, g_exp, g_p = sb("g_z", [P, TC, E]), sb("g_exp", [P, TC, E]), sb("g_p", [P, TC, E])
        g_best = [sb(f"g_best{k}", [P, TC]) for k in range(2)]
        g_first = [sb(f"g_first{k}", [P, TC]) for k in range(2)]
        g_eq = [sb(f"g_eq{k}", [P, TC, E]) for k in range(2)]
        g_rank = [sb(f"g_rank{k}", [P, TC, E]) for k in range(2)]
        g_hot = [sb(f"g_hot{k}", [P, TC, E]) for k in range(2)]
        g_left, g_mask, g_cw = sb("g_left", [P, TC, E]), sb("g_mask", [P, TC, E]), sb("g_cw", [P, TC, E])
        cw_parts = sb("cw_parts", [P, TC, 2, E])

        x2_head = sb("x2_head", [P, C, N], F32R)
        x2_rest = sb("x2_rest", [P, C, N], F32R)
        cw_t = sb("cw_t", [P, C, N], F32R)
        silu = sb("silu", [P, 3, N])
        act = sb("act", [P, 3, N])
        act_head = sb("act_head", [P, 3, N], F32R)
        act_rest = sb("act_rest", [P, 3, N], F32R)
        out_t = sb("out_t", [P, N])

        x_in = [sem(f"x_in{c}") for c in range(C)]
        ctx_in = [sem(f"ctx_in{c}") for c in range(C)]
        attn_w_in, ffn_w_in, small_in, stored = sem("attn_w_in"), sem("ffn_w_in"), sem("small_in"), sem("stored")
        ident_ready, consts_ready, pool_order = sem("ident_ready"), sem("consts_ready"), sem("pool_order")
        w_heads, w_rests = sem("w_heads"), sem("w_rests")
        setup_ps, setup_sb = sem("setup_ps"), sem("setup_sb")
        dve_order = sem("dve_order")
        ln_var, ln_r, xn_ready = [sem("ln1_var"), sem("ln2_var")], [sem("ln1_r"), sem("ln2_r")], [sem("xn1_ready"), sem("xn2_ready")]
        xnt_ps, xnt_sb, ctxt_ps, ctxt_sb = sem("xnt_ps"), sem("xnt_sb"), sem("ctxt_ps"), sem("ctxt_sb")
        t_ps, t_ready, v_ps, v_ready = sem("t_ps"), sem("t_ready"), sem("v_ps"), sem("v_ready")
        sim_ps, simstat_sb, simavg_ps, simavg_sb = sem("sim_ps"), sem("simstat_sb"), sem("simavg_ps"), sem("simavg_sb")
        simvar_sb, simr_sb, negmax_sb = sem("simvar_sb"), sem("simr_sb"), sem("negmax_sb")
        prob_sb, probt_ps, probt_sb, attn_ps, x1_ready = sem("prob_sb"), sem("probt_ps"), sem("probt_sb"), sem("attn_ps"), sem("x1_ready")
        x2t_ps, x2_head_sb, x2_rest_sb = sem("x2t_ps"), sem("x2_head_sb"), sem("x2_rest_sb")
        lg_ps, lg_sb = sem("lg_ps"), sem("lg_sb")
        mask_sb, pick_ready = sem("mask_sb"), sem("pick_ready")
        gz_sb, gexp_sb, cw_sb, cwt_ps, cwt_sb = sem("gz_sb"), sem("gexp_sb"), sem("cw_sb"), sem("cwt_ps"), sem("cwt_sb")
        a_ps, b_ps, cw_ps, silu_sb, scaled_sb = sem("a_ps"), sem("b_ps"), sem("cw_ps"), sem("silu_sb"), sem("scaled_sb")
        act_sb, head_sb, rest_sb, y_ps = sem("act_sb"), sem("head_sb"), sem("rest_sb"), sem("y_ps")
        out_ps, outt_sb, tok_ps, final_sb = sem("out_ps"), sem("outt_sb"), sem("tok_ps"), sem("final_sb")

        x_dram = x.rearrange("b (p i) d -> p b i d", i=IB)
        ctx_dram = ctx.rearrange("b (p i) d -> p b i d", i=IB)
        out_dram = out.rearrange("(c b) (p i) d -> c p b (i d)", i=IB, b=CB)

        def tiles(c):
            return slice(TC * c, TC * (c + 1))

        def per_token(v, shape):
            return v.unsqueeze(2).broadcast_to(shape)

        HID, CW_B, OUT_B, PROB, LATE = bank[0:3], bank[3], bank[4], bank[5:7], bank[7]
        TOKENS = [CW_B, LATE]

        def early(c):
            return bank[3:5] if c == 1 else PROB

        def average(c):
            return bank[1] if c == 1 else LATE

        GROUPS = [(0, 1), (1, 3), (3, 6), (6, NX)]
        ORDER_OF_SPLITS = 2

        def splits_for(e):
            return ORDER_OF_SPLITS + 2 * (1 + next(g for g, (lo, hi) in enumerate(GROUPS) if lo <= e < hi))

        def split_list():
            yield gate_parts[:, 0, :], gate_parts[:, 1, :], gate_w_sb[:, :]
            yield b2_head[:, :], b2_rest[:, :], b2_rows[:, :]
            for lo, hi in GROUPS:
                yield w1_head[:, lo:hi, :], w1_rest[:, lo:hi, :], w1_sb[:, lo:hi, :]
                yield w2_head[:, lo:hi, :], w2_rest[:, lo:hi, :], w2_sb[:, lo:hi, :]

        PE_AT = {'transpose_inputs': [-4, 1], 'project': [-4, 2], 'scores': [-3, 1], 'scores_average': [-1, 4], 'transpose_prob': [1, 3], 'attend': [3, 4], 'transpose_x2': [5, 4], 'router': [7, 0], 'transpose_cw': [10, 3]}
        ACT_AT = {'input_copies': [-4, 1], 'projection_copies': [-4, 1], 'exponentials': [0, 2], 'prob_copies': [2, 2], 'x2_heads': [6, 0], 'router_exp': [9, 1], 'cw_copy': [10, 1]}
        DVE_AT = {'first_statistics': [-8, 0], 'first_normalise': [-6, 0], 'statistics_0': [-4, 2], 'statistics_1': [-2, 0], 'variance': [-1, 1], 'scale': [-1, 2], 'residual': [3, 2], 'second_normalise': [4, 2], 'x2_rests': [5, 1], 'router_logits': [7, 1], 'router_select': [8, 2], 'router_weights': [9, 0]}
        POOL_AT = {'first_rstd': [-9, 1], 'scores_rstd': [-2, 0], 'second_rstd': [4, 0]}

        OPENING = {("exponentials", 1), ("transpose_prob", 1), ("prob_copies", 1), ("router_exp", 0)}

        def due(table, n, place):
            return [(piece, c) for piece, (slot, where) in table.items() for c in range(C)
                    if where == place and (c - 1) * NX + slot == n and (piece, c) not in OPENING]

        def parts(n):
            return [(0, slice(0, N))] if n < NX * C - 1 else [(h, slice(h * N // 2, (h + 1) * N // 2)) for h in range(2)]

        def out_parts(c):
            return parts(NX * (c + 1) - 1)

        block = stack.enter_context(nc.Block())

        @block.sync
        def _(sp):
            def load_x(c):
                sp.dma_start(x_sb[:, tiles(c), :].rearrange("p (b i) d -> p b i d", i=IB),
                             x_dram[:, CB * c:CB * (c + 1)]).then_inc(x_in[c], 16)

            def load_ctx(c):
                sp.dma_start(ctx_sb[:, tiles(c), :].rearrange("p (b i) d -> p b i d", i=IB),
                             ctx_dram[:, CB * c:CB * (c + 1)]).then_inc(ctx_in[c], 16)

            load_x(0)
            for dst, src in ((wq_sb, wq), (wk_sb, wk), (wo_sb, wo), (wv_sb, wv)):
                sp.dma_start(dst[:, :], src).then_inc(attn_w_in, 16)
            load_ctx(0)
            load_x(1)
            load_ctx(1)
            sp.dma_start(b1_rows[0:1, :], sb1).then_inc(small_in, 16)
            sp.dma_start(b1_rows[1:NX, :], rb1).then_inc(small_in, 16)
            sp.dma_start(sb2_col[:, :], sb2.rearrange("a d -> d a")).then_inc(small_in, 16)
            sp.dma_start(gate_b_sb[:, :], gate_b.partition_broadcast(P)).then_inc(small_in, 16)
            sp.wait_ge(consts_ready, 1)
            sp.dma_start(b2_rows[0:E, :], rb2).then_inc(small_in, 16)
            sp.dma_start(b2_rows[E:2 * E, :], rb2).then_inc(small_in, 16)
            sp.dma_start(gate_w_sb[:, :], gate_w).then_inc(small_in, 16)
            sp.dma_start(w1_sb[:, 0, :], sw1[0]).then_inc(ffn_w_in, 16)
            sp.dma_start(w2_sb[:, 0, :], sw2[0]).then_inc(ffn_w_in, 16)
            sp.dma_start(w1_sb[:, 1:NX, :], rw1.rearrange("e d f -> d e f")).then_inc(ffn_w_in, 16)
            sp.dma_start(w2_sb[:, 1:NX, :], rw2.rearrange("e f d -> f e d")).then_inc(ffn_w_in, 16)
            for c in range(2, C):
                load_x(c)
                load_ctx(c)
            for c in range(C):
                if len(out_parts(c)) == 1:
                    sp.wait_ge(final_sb, c + 1)
                    sp.dma_start(out_dram[c], x1[:, tiles(c), :].rearrange("p (b i) d -> p b (i d)", i=IB)).then_inc(stored, 16)
                else:
                    for h in range(CB):
                        t = TC * c + IB * h
                        sp.wait_ge(final_sb, c + 1 + h)
                        sp.dma_start(out_dram[c, :, h], x1[:, t:t + IB, :].rearrange("p i d -> p (i d)")).then_inc(stored, 16)
            sp.wait_ge(stored, 16 * (C + 1))

        @block.gpsimd
        def _(pool):
            order = [0]

            def wait_own(ins):
                order[0] += 1
                ins.then_inc(pool_order, 1)
                pool.wait_ge(pool_order, order[0])

            def rstd(which, c):
                pool.wait_ge(ln_var[which], c + 1)
                if c >= 1:
                    pool.wait_ge(xn_ready[which], c)
                pool.tensor_tensor(ln_rstd[:, which, :], ln_veps[:, which, :], minus_half[:, 0:TC], ALU.pow).then_inc(ln_r[which], 1)

            def scores_rstd(c):
                pool.wait_ge(simvar_sb, c + 1)
                if c >= 1:
                    pool.wait_ge(prob_sb, CB * c)
                pool.tensor_tensor(sim_r[:, :], sim_veps[:, :], minus_half[:, 0:CB], ALU.pow).then_inc(simr_sb, 1)

            def split_rests(lo, hi):
                for k, (head, rest, whole) in enumerate(split_list()):
                    if lo <= k < hi:
                        pool.wait_ge(w_heads, k + 1)
                        pool.tensor_tensor(rest, whole, head.bitcast(F32), ALU.subtract).then_inc(w_rests, 1)

            def expert_rest(c, e):
                n, k = NX * c + e, e % 3
                if n >= 3:
                    pool.wait_ge(y_ps, n - 2)
                for h, cols in parts(n):
                    pool.wait_ge(head_sb, n + 1 + h)
                    pool.tensor_tensor(act_rest[:, k, cols], act[:, k, cols], act_head[:, k, cols].bitcast(F32), ALU.subtract).then_inc(rest_sb, 1)

            wait_own(pool.memset(minus_half[:, :], -0.5))
            wait_own(pool.memset(ident[:, :], 0.0))
            pool.affine_select(out=ident[:, :], in_=ident[:, :], compare_op=ALU.not_equal, fill=1.0, base=0,
                               pattern=[[-1, P]], channel_multiplier=1).then_inc(ident_ready, 1)
            wait_own(pool.memset(b2_rows[:, :], 0.0))
            pool.memset(mean_of_partitions[:, :], 1.0 / P).then_inc(consts_ready, 1)
            rstd(0, 0)
            for k in range(E):
                pool.memset(descending[:, k:k + 1], float(E - k)).then_inc(consts_ready, 1)
            rstd(0, 1)
            pool.memset(cw_t[:, :, :].bitcast(F32), 0.0).then_inc(consts_ready, 1)
            wait_own(pool.memset(pick_f[:, :, :], 0.0))
            for base in (0, -E):
                wait_own(pool.affine_select(out=pick_f[:, :, :], in_=pick_f[:, :, :], compare_op=ALU.not_equal, fill=1.0,
                                            base=base, pattern=[[-1, E], [0, P]], channel_multiplier=1))
            pool.sem_inc(consts_ready, 1)
            scores_rstd(0)
            split_rests(0, 2)
            split_rests(2, 6)
            rstd(1, 0)
            scores_rstd(1)
            pieces = {"first_rstd": lambda c: rstd(0, c), "second_rstd": lambda c: rstd(1, c), "scores_rstd": scores_rstd}
            for n in range(NX * C):
                for piece, c in due(POOL_AT, n, 0):
                    pieces[piece](c)
                if n in (0, 2):
                    split_rests(6 + n, 8 + n)
                expert_rest(n // NX, n % NX)
                for piece, c in due(POOL_AT, n, 1):
                    pieces[piece](c)

        @block.scalar
        def _(scalar):
            copy = scalar.copy

            def xn_copy(c):
                scalar.wait_ge(xnt_ps, c + 1)
                if c >= 1:
                    scalar.wait_ge(t_ps, c)
                copy(xn_t[:, :], early(c)[0][:, :]).then_inc(xnt_sb, 1)

            def ctx_copy(c):
                scalar.wait_ge(ctxt_ps, c + 1)
                if c >= 1:
                    scalar.wait_ge(sim_ps, CB * c)
                copy(ctx_t[:, :], early(c)[1][0:DC, :]).then_inc(ctxt_sb, 1)

            def t_copy(c):
                scalar.wait_ge(t_ps, c + 1)
                if c >= 1:
                    scalar.wait_ge(sim_ps, CB * c)
                copy(t_sb[:, :], early(c)[0][0:DC, :]).then_inc(t_ready, 1)

            def v_copy(c):
                scalar.wait_ge(v_ps, c + 1)
                copy(v_sb[:, c].rearrange("p t d -> p (t d)"), early(c)[1][:, :]).then_inc(v_ready, 1)

            def exponentials(c):
                scalar.wait_ge(negmax_sb, c + 1)
                if c >= 1:
                    scalar.wait_ge(probt_ps, CB * c)
                    scalar.wait_ge(x1_ready, c)
                for j in range(CB):
                    for i in range(IB):
                        last = scalar.activation(prob[:, j, i, :], early(c)[j][:, i * S:(i + 1) * S], ACT.Exp,
                                                 bias=neg_max[:, j, i:i + 1], scale=sim_r[:, j:j + 1],
                                                 accum_out=row_sum[:, j, i:i + 1])
                    last.then_inc(prob_sb, 1)

            def prob_copy(m):
                j = m % CB
                scalar.wait_ge(probt_ps, m + 1)
                if m >= CB:
                    scalar.wait_ge(attn_ps, m // CB)
                copy(prob_t[:, j].rearrange("p k q -> p (k q)"), PROB[j][:, :]).then_inc(probt_sb, 1)

            def x2_heads(c):
                scalar.wait_ge(x2t_ps, c + 1)
                copy(x2_head[:, c, :], LATE[:, :]).then_inc(x2_head_sb, 1)

            def router_exp(c):
                scalar.wait_ge(gz_sb, c + 1)
                if c >= 1:
                    scalar.wait_ge(cw_sb, c)
                scalar.activation(g_exp[:, :, :], g_z[:, :, :], ACT.Exp).then_inc(gexp_sb, 1)

            def cw_copy(c):
                scalar.wait_ge(cwt_ps, c + 1)
                if c == 0:
                    scalar.wait_ge(consts_ready, 2 + E)
                copy(cw_t[0:2 * E, c, :], LATE[0:2 * E, :]).then_inc(cwt_sb, 1)

            def split_heads(lo, hi):
                for k, (head, _, whole) in enumerate(split_list()):
                    if lo <= k < hi:
                        copy(head, whole).then_inc(w_heads, 1)

            def expert_silu(c, e):
                n, k = NX * c + e, e % 3
                scalar.wait_ge(a_ps, n + 1)
                if n >= 3:
                    scalar.wait_ge(act_sb, n - 2)
                for _, cols in parts(n):
                    scalar.activation(silu[:, k, cols], HID[(2 * n) % 3][:, cols], ACT.Silu, bias=b1_cols[:, 0, e:e + 1]).then_inc(silu_sb, 1)

            def expert_head(n):
                k = n % 3
                if n >= 3:
                    scalar.wait_ge(y_ps, n - 2)
                for h, cols in parts(n):
                    scalar.wait_ge(act_sb, n + 1 + h)
                    copy(act_head[:, k, cols], act[:, k, cols]).then_inc(head_sb, 1)

            def out_bias(c):
                scalar.wait_ge(y_ps, NX * (c + 1) + len(out_parts(c)) - 1)
                if c >= 1:
                    scalar.wait_ge(tok_ps, c)
                for _, cols in out_parts(c):
                    scalar.activation(out_t[:, cols], OUT_B[:, cols], ACT.Identity, bias=sb2_col[:, :]).then_inc(outt_sb, 1)

            scalar.wait_ge(setup_ps, 1)
            copy(wo_t[:, :], bank[0][:, 0:D]).then_inc(setup_sb, 1)
            scalar.wait_ge(setup_ps, 2)
            copy(qk_w[:, :], bank[1][:, 0:DC]).then_inc(setup_sb, 1)
            scalar.wait_ge(setup_ps, 3)
            copy(vo_w[:, :], bank[2][0:DC, 0:D]).then_inc(setup_sb, 1)
            ctx_copy(0)
            xn_copy(0)
            v_copy(0)
            t_copy(0)
            xn_copy(1)
            ctx_copy(1)
            t_copy(1)
            v_copy(1)
            exponentials(0)
            scalar.wait_ge(small_in, 16 * 7)
            scalar.wait_ge(setup_ps, 4)
            copy(b1_cols[:, :, :].rearrange("p h e -> p (h e)"), bank[0][:, 0:2 * NX]).then_inc(setup_sb, 1)
            split_heads(0, 2)
            prob_copy(0)
            prob_copy(1)
            scalar.wait_ge(ffn_w_in, 64)
            split_heads(2, 6)
            scalar.wait_ge(consts_ready, 3 + E)
            copy(pick[:, :, :], pick_f[:, :, :]).then_inc(pick_ready, 1)
            split_heads(6, 8)
            x2_heads(0)
            exponentials(1)
            prob_copy(2)
            prob_copy(3)
            router_exp(0)
            split_heads(8, 10)

            def input_copies(c):
                xn_copy(c)
                ctx_copy(c)

            def projection_copies(c):
                t_copy(c)
                v_copy(c)

            def prob_copies(c):
                for j in range(CB):
                    prob_copy(CB * c + j)

            pieces = {"input_copies": input_copies, "projection_copies": projection_copies, "exponentials": exponentials,
                      "prob_copies": prob_copies, "x2_heads": x2_heads,
                      "router_exp": router_exp, "cw_copy": cw_copy}
            for n in range(NX * C):
                c, e = n // NX, n % NX
                if e == 2 and c >= 1:
                    out_bias(c - 1)
                for piece, k in due(ACT_AT, n, 0):
                    pieces[piece](k)
                expert_silu(c, e)
                for piece, k in due(ACT_AT, n, 1):
                    pieces[piece](k)
                if n >= 1:
                    expert_head(n - 1)
                for piece, k in due(ACT_AT, n, 2):
                    pieces[piece](k)
            expert_head(NX * C - 1)
            out_bias(C - 1)

        @block.vector
        def _(dve):
            order = [0]

            def own(ins):
                order[0] += 1
                return ins.then_inc(dve_order, 1)

            def wait_own():
                dve.wait_ge(dve_order, order[0])

            def ln_statistics(which, c, src):
                for i in range(TC):
                    own(dve.bn_stats(ln_stats[:, which, i, :], src[:, TC * c + i, :]))
                wait_own()
                for i in range(TC):
                    own(dve.bn_aggr(ln_mv[:, which, i, :], ln_stats[:, which, i, :]))
                wait_own()
                if c >= 1:
                    dve.wait_ge(ln_r[which], c)
                dve.tensor_scalar(ln_veps[:, which, :], ln_mv[:, which, :, 1], EPS, None, ALU.add).then_inc(ln_var[which], 1)

            def ln_normalise(which, c, src, transposed):
                dve.wait_ge(ln_r[which], c + 1)
                if c >= 1:
                    dve.wait_ge(transposed, c)
                for i in range(TC):
                    last = dve.tensor_scalar(xn[:, which, i, :], src[:, TC * c + i, :], ln_mv[:, which, i, 0:1],
                                             ln_rstd[:, which, i:i + 1], ALU.subtract, ALU.mult)
                last.then_inc(xn_ready[which], 1)

            def scores_statistics(m):
                j = m % CB
                scores = early(m // CB)[j]
                dve.wait_ge(sim_ps, m + 1)
                if m >= CB:
                    dve.wait_ge(negmax_sb, m // CB)
                own(dve.tensor_reduce(row_max[:, j, :], scores[:, :].rearrange("p (i k) -> p i k", i=IB), X, ALU.max))
                own(dve.bn_stats(sim_stats[:, j, :], scores[:, :]))
                wait_own()
                own(dve.bn_aggr(sim_mv[:, j, :], sim_stats[:, j, :]))

            def scores_squares(c):
                wait_own()
                own(dve.tensor_tensor(sim_sq[:, :], sim_mv[:, :, 0], sim_mv[:, :, 0], ALU.mult))
                wait_own()
                dve.tensor_tensor(sim_mv[:, :, 1], sim_sq[:, :], sim_mv[:, :, 1], ALU.add).then_inc(simstat_sb, 1)

            def scores_variance(c):
                dve.wait_ge(simavg_ps, c + 1)
                dve.tensor_copy(sim_avg[:, :, :].rearrange("p j k -> p (j k)"), average(c)[:, 0:2 * CB]).then_inc(simavg_sb, 1)
                dve.wait_ge(simavg_sb, c + 1)
                own(dve.tensor_tensor(sim_sq[:, :], sim_avg[:, :, 0], sim_avg[:, :, 0], ALU.mult))
                wait_own()
                dve.scalar_tensor_tensor(sim_veps[:, :], sim_avg[:, :, 1], EPS, sim_sq[:, :],
                                         ALU.add, ALU.subtract).then_inc(simvar_sb, 1)

            def scores_scale(c):
                dve.wait_ge(simr_sb, c + 1)
                if c >= 1:
                    dve.wait_ge(prob_sb, CB * c)
                for j in range(CB):
                    last = dve.tensor_scalar(neg_max[:, j, :], row_max[:, j, :], sim_r[:, j:j + 1], -1.0, ALU.mult, ALU.mult)
                last.then_inc(negmax_sb, 1)

            def residual(c):
                dve.wait_ge(prob_sb, CB * (c + 1))
                own(dve.reciprocal(row_inv[:, :, :], row_sum[:, :, :]))
                wait_own()
                dve.wait_ge(attn_ps, c + 1)
                for i in range(TC):
                    last = dve.scalar_tensor_tensor(x1[:, TC * c + i, :], LATE[:, i * D:(i + 1) * D],
                                                    row_inv[:, i // IB, i % IB:i % IB + 1], x_sb[:, TC * c + i, :],
                                                    ALU.mult, ALU.add)
                last.then_inc(x1_ready, 1)

            def second_statistics(c):
                dve.wait_ge(x1_ready, c + 1)
                ln_statistics(1, c, x1)

            def x2_rests(c):
                dve.wait_ge(x2_head_sb, c + 1)
                dve.tensor_tensor(x2_rest[:, c, :], LATE[:, :], x2_head[:, c, :].bitcast(F32), ALU.subtract).then_inc(x2_rest_sb, 1)

            full = [P, TC, E]

            def router_logits(c):
                sums = LATE[:, 0:TC * 2 * E].rearrange("p (t h e) -> p t h e", t=TC, h=2)
                if c == 0:
                    dve.wait_ge(small_in, 16 * 7)
                dve.wait_ge(lg_ps, c + 1)
                own(dve.tensor_tensor(logits_part[:, :, :], sums[:, :, 0, :], gate_b_sb[:, :].unsqueeze(1).broadcast_to(full), ALU.add))
                wait_own()
                dve.tensor_tensor(logits[:, :, :], sums[:, :, 1, :], logits_part[:, :, :], ALU.add).then_inc(lg_sb, 1)
                dve.wait_ge(lg_sb, c + 1)
                own(dve.tensor_reduce(g_best[0][:, :], logits[:, :, :], X, ALU.max))
                wait_own()
                if c >= 1:
                    dve.wait_ge(gexp_sb, c)
                dve.tensor_tensor(g_z[:, :, :], logits[:, :, :], per_token(g_best[0][:, :], full), ALU.subtract).then_inc(gz_sb, 1)

            def router_select(c):
                for k, left in enumerate((logits, g_left)):
                    if k == 1:
                        own(dve.scalar_tensor_tensor(g_left[:, :, :], g_hot[0][:, :, :], -3.0e38, logits[:, :, :], ALU.mult, ALU.add))
                        wait_own()
                        own(dve.tensor_reduce(g_best[1][:, :], g_left[:, :, :], X, ALU.max))
                        wait_own()
                    own(dve.tensor_tensor(g_eq[k][:, :, :], left[:, :, :], per_token(g_best[k][:, :], full), ALU.is_ge))
                    wait_own()
                    own(dve.tensor_tensor(g_rank[k][:, :, :], g_eq[k][:, :, :],
                                          descending[:, :].unsqueeze(1).broadcast_to(full), ALU.mult))
                    wait_own()
                    own(dve.tensor_reduce(g_first[k][:, :], g_rank[k][:, :, :], X, ALU.max))
                    wait_own()
                    own(dve.tensor_tensor(g_hot[k][:, :, :], g_rank[k][:, :, :], per_token(g_first[k][:, :], full), ALU.is_equal))
                    wait_own()
                dve.tensor_tensor(g_mask[:, :, :], g_hot[0][:, :, :], g_hot[1][:, :, :], ALU.add).then_inc(mask_sb, 1)

            def router_weights(c):
                dve.wait_ge(gexp_sb, c + 1)
                dve.wait_ge(mask_sb, c + 1)
                own(dve.tensor_reduce(g_sum[:, :], g_exp[:, :, :], X, ALU.add))
                own(dve.tensor_tensor(g_p[:, :, :], g_exp[:, :, :], g_mask[:, :, :], ALU.mult))
                wait_own()
                own(dve.reciprocal(g_inv[:, :], g_sum[:, :]))
                wait_own()
                if c >= 1:
                    dve.wait_ge(cwt_ps, c)
                own(dve.tensor_tensor(cw_parts[:, :, 0, :].bitcast(F32R), g_p[:, :, :], per_token(g_inv[:, :], full), ALU.mult))
                own(dve.tensor_tensor(g_cw[:, :, :], g_p[:, :, :], per_token(g_inv[:, :], full), ALU.mult))
                wait_own()
                dve.tensor_tensor(cw_parts[:, :, 1, :], g_cw[:, :, :], cw_parts[:, :, 0, :], ALU.subtract).then_inc(cw_sb, 1)

            def expert_gate(c, e, between):
                n, k = NX * c + e, e % 3
                for h, cols in parts(n):
                    dve.wait_ge(silu_sb, n + 1 + h)
                    if e >= 1:
                        dve.wait_ge(cw_ps, E * c + e)
                        dve.tensor_tensor(silu[:, k, cols], silu[:, k, cols], CW_B[:, cols], ALU.mult).then_inc(scaled_sb, 1)
                    if h == 0:
                        between()
                    if e >= 1:
                        dve.wait_ge(scaled_sb, E * c + e + h)
                    dve.wait_ge(b_ps, n + 1)
                    if n >= 3:
                        dve.wait_ge(rest_sb, n - 2)
                    dve.scalar_tensor_tensor(act[:, k, cols], HID[(2 * n + 1) % 3][:, cols], b1_cols[:, 1, e:e + 1], silu[:, k, cols],
                                             ALU.add, ALU.mult).then_inc(act_sb, 1)

            def final(c):
                rows = x1[:, tiles(c), :].rearrange("p t d -> p (t d)")
                for h, cols in out_parts(c):
                    dve.wait_ge(tok_ps, c + 1 + h)
                    dve.tensor_tensor(rows[:, cols], TOKENS[h][:, cols], rows[:, cols], ALU.add).then_inc(final_sb, 1)

            for c in range(2):
                dve.wait_ge(x_in[c], 16)
                ln_statistics(0, c, x_sb)
                ln_normalise(0, c, x_sb, xnt_ps)
            scores_statistics(0)
            scores_statistics(1)
            scores_squares(0)
            scores_variance(0)
            scores_scale(0)
            scores_statistics(CB)
            scores_statistics(CB + 1)
            scores_squares(1)
            residual(0)
            second_statistics(0)
            scores_variance(1)
            ln_normalise(1, 0, x1, x2t_ps)
            scores_scale(1)
            x2_rests(0)
            dve.wait_ge(consts_ready, 1 + E)
            router_logits(0)
            router_select(0)
            dve.wait_ge(setup_sb, 4)

            def first_statistics(c):
                dve.wait_ge(x_in[c], 16)
                ln_statistics(0, c, x_sb)

            def attention_output(c):
                residual(c)
                second_statistics(c)

            def statistics_1(c):
                scores_statistics(CB * c + 1)
                scores_squares(c)

            pieces = {"first_statistics": first_statistics, "first_normalise": lambda c: ln_normalise(0, c, x_sb, xnt_ps),
                      "statistics_0": lambda c: scores_statistics(CB * c), "statistics_1": statistics_1,
                      "variance": scores_variance, "scale": scores_scale, "residual": attention_output,
                      "second_normalise": lambda c: ln_normalise(1, c, x1, x2t_ps), "x2_rests": x2_rests,
                      "router_logits": router_logits, "router_select": router_select, "router_weights": router_weights}

            def run(n, place):
                for piece, c in due(DVE_AT, n, place):
                    pieces[piece](c)

            for n in range(NX * C):
                c, e = n // NX, n % NX
                if e == 3 and c >= 1:
                    final(c - 1)
                run(n, 0)
                expert_gate(c, e, lambda: run(n, 1))
                run(n, 2)
            final(C - 1)

        @block.tensor
        def _(pe):
            def mm(dst, lhs, rhs, start=True, stop=True):
                return pe.matmul(dst, lhs, rhs, start=start, stop=stop, skip_group_check=True)

            def transpose_x(c):
                pe.wait_ge(xn_ready[0], c + 1)
                if c >= 2:
                    pe.wait_ge(probt_sb, CB * c - 1)
                for i in range(TC):
                    last = pe.transpose(early(c)[0][:, i * P:(i + 1) * P], xn[:, 0, i, :], ident[:, :])
                last.then_inc(xnt_ps, 1)

            def transpose_ctx(c):
                pe.wait_ge(ctx_in[c], 16)
                if c >= 2:
                    pe.wait_ge(probt_sb, CB * c)
                for i in range(TC):
                    last = pe.transpose(early(c)[1][0:DC, i * P:(i + 1) * P], ctx_sb[:, TC * c + i, :], ident[:, :])
                last.then_inc(ctxt_ps, 1)

            def project_q(c):
                pe.wait_ge(xnt_sb, c + 1)
                mm(early(c)[0][0:DC, :], qk_w[:, :], xn_t[:, :]).then_inc(t_ps, 1)

            def project_v(c):
                pe.wait_ge(ctxt_sb, c + 1)
                for i in range(TC):
                    last = mm(early(c)[1][:, i * D:(i + 1) * D], ctx_t[:, i * P:(i + 1) * P], vo_w[:, :])
                last.then_inc(v_ps, 1)

            def scores(c):
                pe.wait_ge(t_ready, c + 1)
                pe.wait_ge(ctxt_sb, c + 1)
                pe.wait_ge(v_ready, c + 1)
                for j in range(CB):
                    for i in range(IB):
                        q = (IB * j + i) * P
                        last = mm(early(c)[j][:, i * S:(i + 1) * S], t_sb[:, q:q + P], ctx_t[:, j * S:(j + 1) * S])
                    last.then_inc(sim_ps, 1)

            def scores_average(c):
                pe.wait_ge(simstat_sb, c + 1)
                if c == 0:
                    pe.wait_ge(consts_ready, 1)
                elif c == 1:
                    pe.wait_ge(setup_sb, 2)
                else:
                    pe.wait_ge(lg_sb, c)
                mm(average(c)[:, 0:2 * CB], mean_of_partitions[:, :], sim_mv[:, :, :].rearrange("p j k -> p (j k)")).then_inc(simavg_ps, 1)

            def transpose_prob(c):
                pe.wait_ge(prob_sb, CB * (c + 1))
                for j in range(CB):
                    for k in range(IB):
                        for i in range(IB):
                            last = pe.transpose(PROB[j][:, k * S + i * P:k * S + (i + 1) * P],
                                                prob[:, j, i, k * P:(k + 1) * P], ident[:, :])
                    last.then_inc(probt_ps, 1)

            def attend(c):
                pe.wait_ge(v_ready, c + 1)
                if c >= 1:
                    pe.wait_ge(cwt_sb, c)
                for j in range(CB):
                    pe.wait_ge(probt_sb, CB * c + j + 1)
                    for i in range(IB):
                        for k in range(IB):
                            last = mm(LATE[:, (IB * j + i) * D:(IB * j + i + 1) * D], prob_t[:, j, k, i * P:(i + 1) * P],
                                      v_sb[:, c, IB * j + k, :], start=k == 0, stop=k == IB - 1)
                last.then_inc(attn_ps, 1)

            def transpose_x2(c):
                pe.wait_ge(xn_ready[1], c + 1)
                pe.wait_ge(x1_ready, c + 1)
                for i in range(TC):
                    last = pe.transpose(LATE[:, i * P:(i + 1) * P], xn[:, 1, i, :], ident[:, :])
                last.then_inc(x2t_ps, 1)

            def router(c):
                pe.wait_ge(x2_head_sb, c + 1)
                pe.wait_ge(x2_rest_sb, c + 1)
                if c == 0:
                    pe.wait_ge(w_rests, 1)
                for i in range(TC):
                    for k, xs in enumerate((x2_head, x2_rest)):
                        last = mm(LATE[:, i * 2 * E:(i + 1) * 2 * E], xs[:, c, i * P:(i + 1) * P],
                                  gate_parts[:, :, :].rearrange("p h e -> p (h e)"), start=k == 0, stop=k == 1)
                last.then_inc(lg_ps, 1)

            def transpose_cw(c):
                pe.wait_ge(cw_sb, c + 1)
                pe.wait_ge(lg_sb, c + 1)
                if 2 <= c + 1 < C:
                    pe.wait_ge(simavg_sb, c + 2)
                for i in range(TC):
                    last = pe.transpose(LATE[0:2 * E, i * P:(i + 1) * P], cw_parts[:, i].rearrange("p h e -> p (h e)"), ident[:, :])
                last.then_inc(cwt_ps, 1)

            def hidden(c, e, half):
                n = NX * c + e
                dst = HID[(2 * n + half) % 3]
                cols = slice(half * FF, (half + 1) * FF)
                if half == 0 and n >= 2:
                    pe.wait_ge(act_sb, n - 1)
                if half == 1 and n >= 1:
                    pe.wait_ge(silu_sb, n)
                mm(dst[:, :], w1_head[:, e, cols], x2_head[:, c, :], True, False)
                mm(dst[:, :], w1_head[:, e, cols], x2_rest[:, c, :], False, False)
                mm(dst[:, :], w1_rest[:, e, cols], x2_head[:, c, :], False, True).then_inc((a_ps, b_ps)[half], 1)

            def spread_cw(c, e):
                if E * c + e == 1:
                    pe.wait_ge(prob_sb, 2 * CB)
                else:
                    pe.wait_ge(scaled_sb, E * c + e - 1)
                if e == 1:
                    pe.wait_ge(cwt_sb, c + 1)
                    if c == 0:
                        pe.wait_ge(pick_ready, 1)
                if e == 3 and c >= 1:
                    pe.wait_ge(final_sb, c)
                mm(CW_B[:, :], pick[:, e - 1, :], cw_t[:, c, :]).then_inc(cw_ps, 1)

            def down(n):
                c, e, k = n // NX, n % NX, n % 3
                if e == 0 and c >= 1:
                    pe.wait_ge(outt_sb, c)
                if e == 1:
                    if c == 0:
                        pe.wait_ge(w_rests, 2)
                    mm(OUT_B[:, :], b2_head[:, :], cw_t[:, c, :], False, False)
                    mm(OUT_B[:, :], b2_rest[:, :], cw_t[:, c, :], False, False)
                for h, cols in parts(n):
                    pe.wait_ge(head_sb, n + 1 + h)
                    mm(OUT_B[:, cols], w2_head[:, e, :], act_head[:, k, cols], e == 0, False)
                    mm(OUT_B[:, cols], w2_rest[:, e, :], act_head[:, k, cols], False, False)
                    pe.wait_ge(rest_sb, n + 1 + h)
                    mm(OUT_B[:, cols], w2_head[:, e, :], act_rest[:, k, cols], False, e == NX - 1).then_inc(y_ps, 1)

            def to_tokens(c, cw_used):
                pe.wait_ge(scaled_sb, cw_used)
                for h, cols in out_parts(c):
                    pe.wait_ge(outt_sb, c + 1 + h)
                    for i in range(cols.start // P, cols.stop // P):
                        last = pe.transpose(TOKENS[h][:, i * P:(i + 1) * P], out_t[:, i * P:(i + 1) * P], ident[:, :])
                    last.then_inc(tok_ps, 1)

            pe.wait_ge(ident_ready, 1)
            pe.wait_ge(attn_w_in, 64)
            pe.transpose(bank[0][:, 0:D], wo_sb[:, :], ident[:, :]).then_inc(setup_ps, 1)
            mm(bank[1][:, 0:DC], wq_sb[:, :], wk_sb[:, :]).then_inc(setup_ps, 1)
            pe.wait_ge(setup_sb, 1)
            mm(bank[2][0:DC, 0:D], wv_sb[:, :], wo_t[:, :]).then_inc(setup_ps, 1)
            transpose_ctx(0)
            transpose_x(0)
            pe.wait_ge(setup_sb, 3)
            project_v(0)
            project_q(0)
            scores(0)
            transpose_x(1)
            transpose_ctx(1)
            project_q(1)
            scores_average(0)
            project_v(1)
            scores(1)
            pe.wait_ge(small_in, 16 * 7)
            for h in range(2):
                last = pe.transpose(bank[0][:, h * NX:(h + 1) * NX], b1_rows[:, h * FF:(h + 1) * FF], ident[0:NX, 0:NX])
            last.then_inc(setup_ps, 1)
            transpose_prob(0)
            attend(0)
            scores_average(1)
            transpose_x2(0)
            router(0)
            transpose_prob(1)
            pe.wait_ge(setup_sb, 4)

            def transpose_inputs(c):
                transpose_x(c)
                transpose_ctx(c)

            def project(c):
                project_q(c)
                project_v(c)

            pieces = {"transpose_inputs": transpose_inputs, "project": project, "scores": scores,
                      "scores_average": scores_average, "transpose_prob": transpose_prob, "attend": attend,
                      "transpose_x2": transpose_x2, "router": router, "transpose_cw": transpose_cw}

            def run(n, place):
                for piece, c in due(PE_AT, n, place):
                    pieces[piece](c)

            for n in range(NX * C):
                c, e = n // NX, n % NX
                if c == 0:
                    pe.wait_ge(w_rests, splits_for(e))
                run(n, 0)
                hidden(c, e, 0)
                if e == 3 and c >= 1:
                    to_tokens(c - 1, E * c + e - 1)
                run(n, 1)
                hidden(c, e, 1)
                run(n, 2)
                if e not in (0, 1, 3):
                    spread_cw(c, e)
                run(n, 3)
                if n >= 2:
                    down(n - 2)
                if e in (1, 3):
                    spread_cw(c, e)
                run(n, 4)
            down(NX * C - 2)
            down(NX * C - 1)
            to_tokens(C - 1, E * C + 1)


_INS = ['x', 'ctx_768', 'L0_xattn_Wq', 'L0_xattn_Wk', 'L0_xattn_Wv', 'L0_xattn_Wo', 'L0_ffn_gate_w', 'L0_ffn_gate_b',
        'L0_ffn_sw1', 'L0_ffn_sb1', 'L0_ffn_sw2', 'L0_ffn_sb2', 'L0_ffn_rw1', 'L0_ffn_rb1', 'L0_ffn_rw2', 'L0_ffn_rb2']
_OUTS = [((8, 256, 128), 'float32')]


def kernel(**inputs):
    import numpy as _np
    import concourse.bacc as _bacc
    from concourse import mybir as _mybir
    from concourse.bass_utils import run_bass_kernel_spmd as _run

    nc = _bacc.Bacc("TRN2", target_bir_lowering=False, num_devices=1)
    arrays, args = {}, []
    for name in _INS:
        a = _np.ascontiguousarray(inputs[name])
        arrays[f"in_{name}_dram"] = a
        args.append(nc.dram_tensor(f"in_{name}_dram", a.shape, _mybir.dt.from_np(a.dtype), kind="ExternalInput").ap())
    for i, (shape, dtype) in enumerate(_OUTS):
        dt = _mybir.dt.from_np(_np.dtype(dtype))
        args.append(nc.dram_tensor(f"out_{i}_dram", shape, dt, kind="ExternalOutput").ap())
    xattn_moe_kernel(nc, *args)
    r = _run(nc, [arrays], core_ids=[0])
    got = tuple(r.results[0][f"out_{i}_dram"] for i in range(len(_OUTS)))
    return got[0]
```
